# Optimizing a Trainium2 kernel written in Bass

```python
import numpy as np
import jax
import jax.numpy as jnp

def _softmax(x, axis=-1):
    return jax.nn.softmax(x, axis=axis)

def _gelu(x):
    return jax.nn.gelu(x, approximate=True)

def _silu(x):
    return jax.nn.silu(x)

def _sigmoid(x):
    return jax.nn.sigmoid(x)

def _layernorm(x, axis=-1, eps=1e-05):
    m = jnp.mean(x, axis=axis, keepdims=True)
    v = jnp.var(x, axis=axis, keepdims=True)
    return (x - m) / jnp.sqrt(v + eps)

def _scatter_add(tgt, idx, src, axis=0):
    return tgt.at[idx].add(src)

def _segment_sum(src, seg, n):
    return jax.ops.segment_sum(src, seg, n)
kernel_name = 'mk_gnn_resnorm_d4_gnn_r32_e8458f'

def setup_inputs(seed: int=0):
    np.random.seed(seed)
    _w = jnp.asarray

    def _rec_inputs():
        import jax
        import jax.numpy as jnp
        _gk = jax.random.key(seed)
        x = -0.0005207 + 1.001 * jax.random.normal(jax.random.fold_in(_gk, 1), (128, 512), jnp.float32)
        _s = jax.random.randint(jax.random.fold_in(_gk, 2), (1024,), 0, 128, jnp.int32)
        _d = jax.random.randint(jax.random.fold_in(_gk, 3), (1024,), 0, 128, jnp.int32)
        _loop = jnp.arange(128, dtype=jnp.int32)
        src = jnp.concatenate([_s, _d, _loop])
        dst = jnp.concatenate([_d, _s, _loop])
        _o = jnp.argsort(dst, stable=True)
        src = src[_o]
        dst = dst[_o]
        return (x, src, dst)
    x, src, dst = _rec_inputs()

    def _L0_gnn_setup():
        import jax, jax.numpy as jnp
        import numpy as np
        N, D, H, E = (128, 512, 8, 4096)
        DH = D // H
        EPS = 1e-05
        NEG = -1000000000.0

        def layer_norm(x, w, b):
            m = jnp.mean(x, axis=-1, keepdims=True)
            v = jnp.mean((x - m) ** 2, axis=-1, keepdims=True)
            return (x - m) * jax.lax.rsqrt(v + EPS) * w + b
        key = jax.random.key(seed)
        ks = jax.random.split(key, 10)
        s = 0.02
        return {'x': jax.random.normal(ks[0], (N, D), dtype=jnp.float32), 'edge_index': jax.random.randint(ks[1], (2, E), 0, N, dtype=jnp.int64), 'ln1_w': jnp.ones((D,), jnp.float32), 'ln1_b': jnp.zeros((D,), jnp.float32), 'w_in': jax.random.normal(ks[2], (3 * D, D), jnp.float32) * s, 'b_in': jnp.zeros((3 * D,), jnp.float32), 'w_out': jax.random.normal(ks[3], (D, D), jnp.float32) * s, 'b_out': jnp.zeros((D,), jnp.float32), 'ln2_w': jnp.ones((D,), jnp.float32), 'ln2_b': jnp.zeros((D,), jnp.float32), 'w1': jax.random.normal(ks[4], (4 * D, D), jnp.float32) * s, 'b1': jnp.zeros((4 * D,), jnp.float32), 'w2': jax.random.normal(ks[5], (D, 4 * D), jnp.float32) * s, 'b2': jnp.zeros((D,), jnp.float32)}
    _L0_gnn_all = _L0_gnn_setup()
    _L0_gnn_in = {k: v for k, v in _L0_gnn_all.items() if k in ('ln1_w', 'ln1_b', 'w_in', 'b_in', 'w_out', 'b_out', 'ln2_w', 'ln2_b', 'w1', 'b1', 'w2', 'b2')}
    del _L0_gnn_all

    def _L1_gnn_setup():
        import jax, jax.numpy as jnp
        import numpy as np
        N_NODES = 10000
        N_EDGES = 5000
        IN_DIM = 512
        OUT_DIM = 512
        LN_EPS = 1e-05
        key = jax.random.key(seed)
        k_x, k_src, k_ws, k_wn = jax.random.split(key, 4)
        x = jax.random.normal(k_x, (N_NODES, IN_DIM), dtype=jnp.float32)
        edge_src = jax.random.randint(k_src, (N_EDGES,), 0, N_NODES, dtype=jnp.int32)
        edge_dst = jnp.repeat(jnp.arange(N_NODES, dtype=jnp.int32), N_EDGES // N_NODES)
        deg = jnp.full((N_NODES,), float(N_EDGES // N_NODES), dtype=jnp.float32)
        scale = 1.0 / np.sqrt(IN_DIM)
        W_self = jax.random.normal(k_ws, (OUT_DIM, IN_DIM), dtype=jnp.float32) * scale
        W_neigh = jax.random.normal(k_wn, (OUT_DIM, IN_DIM), dtype=jnp.float32) * scale
        bias = jnp.zeros((OUT_DIM,), dtype=jnp.float32)
        gamma = jnp.ones((OUT_DIM,), dtype=jnp.float32)
        beta = jnp.zeros((OUT_DIM,), dtype=jnp.float32)
        return {'x': x, 'edge_src': edge_src, 'edge_dst': edge_dst, 'deg': deg, 'W_self': W_self, 'W_neigh': W_neigh, 'bias': bias, 'gamma': gamma, 'beta': beta}
    _L1_gnn_all = _L1_gnn_setup()
    _L1_gnn_in = {k: v for k, v in _L1_gnn_all.items() if k in ('W_self', 'W_neigh', 'bias', 'gamma', 'beta')}
    del _L1_gnn_all

    def _L2_gnn_setup():
        import jax, jax.numpy as jnp
        import numpy as np
        N, E, F, H, L = (10000, 5000, 512, 512, 5)

        def _gin_layer(h, src, dst, W, b, e, num_nodes):
            agg = jax.ops.segment_sum(h[src], dst, num_segments=num_nodes)
            z = (1.0 + e) * h + agg
            return jax.nn.relu(z @ W + b)
        key = jax.random.key(seed)
        ks = jax.random.split(key, 6)
        x = jax.random.normal(ks[0], (N, F), dtype=jnp.float32)
        edge_index = jax.random.randint(ks[1], (2, E), 0, N, dtype=jnp.int64)
        W1 = jax.random.normal(ks[2], (F, H), dtype=jnp.float32) * (1.0 / np.sqrt(F))
        b1 = jnp.zeros((H,), dtype=jnp.float32)
        Ws = jax.random.normal(ks[3], (L - 1, H, H), dtype=jnp.float32) * (1.0 / np.sqrt(H))
        bs = jnp.zeros((L - 1, H), dtype=jnp.float32)
        eps = jnp.zeros((L,), dtype=jnp.float32)
        return {'x': x, 'edge_index': edge_index, 'W1': W1, 'b1': b1, 'Ws': Ws, 'bs': bs, 'eps': eps}
    _L2_gnn_all = _L2_gnn_setup()
    _L2_gnn_in = {k: v for k, v in _L2_gnn_all.items() if k in ('W1', 'b1', 'Ws', 'bs', 'eps')}
    del _L2_gnn_all

    def _L3_gnn_setup():
        import jax, jax.numpy as jnp
        import numpy as np
        N_NODES = 3125
        N_EDGES = 25000
        DIM = 512
        key = jax.random.key(seed)
        k1, k2, k3, k4 = jax.random.split(key, 4)
        scale = 1.0 / np.sqrt(DIM)
        embedding = jax.random.normal(k1, (N_NODES, DIM), dtype=jnp.float32)
        edge_index = jax.random.randint(k2, (2, N_EDGES), 0, N_NODES, dtype=jnp.int64)
        W_gcn = jax.random.normal(k3, (DIM, DIM), dtype=jnp.float32) * scale
        b_gcn = jnp.zeros((DIM,), dtype=jnp.float32)
        W_dense = jax.random.normal(k4, (DIM, DIM), dtype=jnp.float32) * scale
        b_dense = jnp.zeros((DIM,), dtype=jnp.float32)
        return {'embedding': embedding, 'edge_index': edge_index, 'W_gcn': W_gcn, 'b_gcn': b_gcn, 'W_dense': W_dense, 'b_dense': b_dense}
    _L3_gnn_all = _L3_gnn_setup()
    _L3_gnn_in = {k: v for k, v in _L3_gnn_all.items() if k in ('W_gcn', 'b_gcn', 'W_dense', 'b_dense')}
    del _L3_gnn_all
    return {'x': x, 'src': src, 'dst': dst, 'L0_gnn_ln1_w': _L0_gnn_in['ln1_w'], 'L0_gnn_ln1_b': _L0_gnn_in['ln1_b'], 'L0_gnn_w_in': _L0_gnn_in['w_in'], 'L0_gnn_b_in': _L0_gnn_in['b_in'], 'L0_gnn_w_out': _L0_gnn_in['w_out'], 'L0_gnn_b_out': _L0_gnn_in['b_out'], 'L0_gnn_ln2_w': _L0_gnn_in['ln2_w'], 'L0_gnn_ln2_b': _L0_gnn_in['ln2_b'], 'L0_gnn_w1': _L0_gnn_in['w1'], 'L0_gnn_b1': _L0_gnn_in['b1'], 'L0_gnn_w2': _L0_gnn_in['w2'], 'L0_gnn_b2': _L0_gnn_in['b2'], 'L1_gnn_W_self': _L1_gnn_in['W_self'], 'L1_gnn_W_neigh': _L1_gnn_in['W_neigh'], 'L1_gnn_bias': _L1_gnn_in['bias'], 'L1_gnn_gamma': _L1_gnn_in['gamma'], 'L1_gnn_beta': _L1_gnn_in['beta'], 'L2_gnn_W1': _L2_gnn_in['W1'], 'L2_gnn_b1': _L2_gnn_in['b1'], 'L2_gnn_Ws': _L2_gnn_in['Ws'], 'L2_gnn_bs': _L2_gnn_in['bs'], 'L2_gnn_eps': _L2_gnn_in['eps'], 'L3_gnn_W_gcn': _L3_gnn_in['W_gcn'], 'L3_gnn_b_gcn': _L3_gnn_in['b_gcn'], 'L3_gnn_W_dense': _L3_gnn_in['W_dense'], 'L3_gnn_b_dense': _L3_gnn_in['b_dense']}

def reference(x, src, dst, L0_gnn_ln1_w, L0_gnn_ln1_b, L0_gnn_w_in, L0_gnn_b_in, L0_gnn_w_out, L0_gnn_b_out, L0_gnn_ln2_w, L0_gnn_ln2_b, L0_gnn_w1, L0_gnn_b1, L0_gnn_w2, L0_gnn_b2, L1_gnn_W_self, L1_gnn_W_neigh, L1_gnn_bias, L1_gnn_gamma, L1_gnn_beta, L2_gnn_W1, L2_gnn_b1, L2_gnn_Ws, L2_gnn_bs, L2_gnn_eps, L3_gnn_W_gcn, L3_gnn_b_gcn, L3_gnn_W_dense, L3_gnn_b_dense):
    import jax
    import jax.numpy as jnp

    def _L0_gnn_ref(x, edge_index, ln1_w, ln1_b, w_in, b_in, w_out, b_out, ln2_w, ln2_b, w1, b1, w2, b2):
        import jax, jax.numpy as jnp
        import numpy as np
        N, D, H, E = (128, 512, 8, 4096)
        DH = D // H
        EPS = 1e-05
        NEG = -1000000000.0

        def layer_norm(x, w, b):
            m = jnp.mean(x, axis=-1, keepdims=True)
            v = jnp.mean((x - m) ** 2, axis=-1, keepdims=True)
            return (x - m) * jax.lax.rsqrt(v + EPS) * w + b
        n = x.shape[0]
        adj = jnp.zeros((n, n), dtype=bool)
        adj = adj.at[edge_index[0], edge_index[1]].set(True)
        adj = adj.at[jnp.arange(n), jnp.arange(n)].set(True)
        add_mask = jnp.where(adj, 0.0, NEG).astype(x.dtype)
        xn = layer_norm(x, ln1_w, ln1_b)
        qkv = xn @ w_in.T + b_in
        q, k, v = jnp.split(qkv, 3, axis=-1)
        q = q.reshape(n, H, DH).transpose(1, 0, 2)
        k = k.reshape(n, H, DH).transpose(1, 0, 2)
        v = v.reshape(n, H, DH).transpose(1, 0, 2)
        scores = jnp.einsum('hqd,hkd->hqk', q, k) / jnp.sqrt(jnp.asarray(DH, x.dtype))
        scores = scores + add_mask[None]
        attn = jax.nn.softmax(scores, axis=-1)
        o = jnp.einsum('hqk,hkd->hqd', attn, v)
        o = o.transpose(1, 0, 2).reshape(n, D)
        attn_out = o @ w_out.T + b_out
        x = x + attn_out
        xm = layer_norm(x, ln2_w, ln2_b)
        mlp = jax.nn.relu(xm @ w1.T + b1) @ w2.T + b2
        return x + mlp

    def _L1_gnn_ref(x, edge_src, edge_dst, deg, W_self, W_neigh, bias, gamma, beta):
        import jax, jax.numpy as jnp
        import numpy as np
        N_NODES = 10000
        N_EDGES = 5000
        IN_DIM = 512
        OUT_DIM = 512
        LN_EPS = 1e-05
        n = x.shape[0]
        h_self = jnp.einsum('nd,od->no', x, W_self)
        neigh_sum = jax.ops.segment_sum(x[edge_src], edge_dst, num_segments=n)
        neigh_mean = neigh_sum / jnp.maximum(deg, 1.0)[:, None]
        h_neigh = jnp.einsum('nd,od->no', neigh_mean, W_neigh)
        h = h_self + h_neigh + bias
        mu = jnp.mean(h, axis=-1, keepdims=True)
        var = jnp.mean(jnp.square(h - mu), axis=-1, keepdims=True)
        h = (h - mu) * jax.lax.rsqrt(var + LN_EPS)
        return h * gamma + beta

    def _L2_gnn_ref(x, edge_index, W1, b1, Ws, bs, eps):
        import jax, jax.numpy as jnp
        import numpy as np
        N, E, F, H, L = (10000, 5000, 512, 512, 5)

        def _gin_layer(h, src, dst, W, b, e, num_nodes):
            agg = jax.ops.segment_sum(h[src], dst, num_segments=num_nodes)
            z = (1.0 + e) * h + agg
            return jax.nn.relu(z @ W + b)
        src, dst = (edge_index[0], edge_index[1])
        num_nodes = x.shape[0]
        h = _gin_layer(x, src, dst, W1, b1, eps[0], num_nodes)
        for i in range(Ws.shape[0]):
            h = _gin_layer(h, src, dst, Ws[i], bs[i], eps[i + 1], num_nodes)
        return jax.nn.log_softmax(h, axis=1)

    def _L3_gnn_ref(embedding, edge_index, W_gcn, b_gcn, W_dense, b_dense):
        import jax, jax.numpy as jnp
        import numpy as np
        N_NODES = 3125
        N_EDGES = 25000
        DIM = 512
        N = embedding.shape[0]
        loop = jnp.arange(N, dtype=edge_index.dtype)
        src = jnp.concatenate([edge_index[0], loop])
        dst = jnp.concatenate([edge_index[1], loop])
        deg = jax.ops.segment_sum(jnp.ones_like(dst, dtype=embedding.dtype), dst, num_segments=N)
        dinv = jnp.where(deg > 0, jax.lax.rsqrt(deg), 0.0)
        norm = dinv[src] * dinv[dst]
        h = embedding @ W_gcn
        msg = h[src] * norm[:, None]
        agg = jax.ops.segment_sum(msg, dst, num_segments=N) + b_gcn
        return agg @ W_dense + b_dense
    edge_index = jnp.stack([src, dst])
    deg = jnp.maximum(jax.ops.segment_sum(jnp.ones(dst.shape, jnp.float32), dst, num_segments=128), 1.0)
    x = _layernorm(x + _L0_gnn_ref(x, edge_index, L0_gnn_ln1_w, L0_gnn_ln1_b, L0_gnn_w_in, L0_gnn_b_in, L0_gnn_w_out, L0_gnn_b_out, L0_gnn_ln2_w, L0_gnn_ln2_b, L0_gnn_w1, L0_gnn_b1, L0_gnn_w2, L0_gnn_b2), axis=-1)
    x = _layernorm(x + _L1_gnn_ref(x, src, dst, deg, L1_gnn_W_self, L1_gnn_W_neigh, L1_gnn_bias, L1_gnn_gamma, L1_gnn_beta), axis=-1)
    x = _layernorm(x + _L2_gnn_ref(x, edge_index, L2_gnn_W1, L2_gnn_b1, L2_gnn_Ws, L2_gnn_bs, L2_gnn_eps), axis=-1)
    x = _layernorm(x + _L3_gnn_ref(x, edge_index, L3_gnn_W_gcn, L3_gnn_b_gcn, L3_gnn_W_dense, L3_gnn_b_dense), axis=-1)
    return x

_drawn_inputs = setup_inputs


def setup_inputs(seed=0):
    import zlib

    import numpy as np

    out = dict(_drawn_inputs(seed))
    spreads = {'L0_gnn_ln1_w': (1.0, 0.6),
     'L0_gnn_ln1_b': (0.0, 0.1),
     'L0_gnn_b_in': (0.0, 0.1),
     'L0_gnn_b_out': (0.0, 0.1),
     'L0_gnn_ln2_w': (1.0, 0.6),
     'L0_gnn_ln2_b': (0.0, 0.1),
     'L0_gnn_b1': (0.0, 0.1),
     'L0_gnn_b2': (0.0, 0.1),
     'L1_gnn_bias': (0.0, 0.1),
     'L1_gnn_gamma': (1.0, 0.2),
     'L1_gnn_beta': (0.0, 0.1),
     'L2_gnn_b1': (0.0, 0.502),
     'L2_gnn_bs': (0.0, 0.8),
     'L2_gnn_eps': (0.0, 0.8),
     'L3_gnn_b_gcn': (0.0, 0.1),
     'L3_gnn_b_dense': (0.0, 0.1)}
    factors = {}
    for name, (base, spread) in spreads.items():
        noise = np.random.default_rng([zlib.crc32(name.encode()), seed]).standard_normal(out[name].shape)
        drawn = base * np.exp(spread * noise) if base else spread * noise
        out[name] = jnp.asarray(drawn.astype(out[name].dtype))
    for name, factor in factors.items():
        out[name] = (out[name] * factor).astype(out[name].dtype)
    return out
```

```python
from contextlib import ExitStack

import concourse.bass as bass
from concourse import mybir

ALU = mybir.AluOpType
ACT = mybir.ActivationFunctionType
F32 = mybir.dt.float32
BF16 = mybir.dt.bfloat16
I32 = mybir.dt.int32
AX_X = mybir.AxisListType.X

P = 128
D = 512
C = D // P
HALF = D // 2
HEADS = 8
DH = D // HEADS
FF = 4 * D
EDGES = 2 * 1024 + P
EC = EDGES // P
GIN = 5
LN_EPS = 1e-5
NEG = 1e9
RING = 14

GROUPS = (["q", "k", "v", "out"] + [f"up{j}" for j in range(4)] + [f"down{j}" for j in range(4)]
          + ["self", "neigh"] + [f"gin{i}" for i in range(GIN)] + ["gcn", "dense"])
G = {name: i for i, name in enumerate(GROUPS)}
PIECES = {"q": 4, "k": 2, "v": 2}

COLS = [("ln1_w", C), ("ln1_b", C), ("b_q", C), ("b_k", C), ("ln2_w", C), ("ln2_b", C), ("b_up", FF // P), ("b_gcn", C)]
COL = {}
for _name, _n in COLS:
    COL[_name] = sum(n for m, n in COLS[:[m for m, _ in COLS].index(_name)])
NCOL = sum(n for _, n in COLS)
ROWS = ["b_v", "b_out", "b_down", "gamma", "beta", "b_dense"]
ROW = {name: i for i, name in enumerate(ROWS)}
BIAS = ["l1"] + [f"gin{i}" for i in range(GIN)]

HEAD_ORDER = [0, 2, 1, 3, 4, 6, 5, 7]

LN1, LN2, LNX1, LNH, LNX2, LNX3, LNX4 = range(7)
(T_LN1, T_Q, T_K, T_O, T_LN2, T_UP, T_X1, T_GIN, T_X3, T_AGG) = (1, 2, 3, 4, 5, 6, 10, 11, 16, 17)
(R_OUT, R_DOWN, R_L1, R_GIN, R_GCN, R_DENSE) = (1, 2, 3, 4, 9, 10)


def residual_gnn(nc, x, edges, cols, rows, bias_rows, eps, weights, out):
    with ExitStack() as ctx:
        def sb(name, shape, dt=F32):
            return ctx.enter_context(nc.sbuf_tensor(name, shape, dt))

        def sem(name):
            return ctx.enter_context(nc.semaphore(name))

        bank = [ctx.enter_context(nc.psum_tensor(f"bank{i}", [P, 512], F32)) for i in range(8)]
        T, R, U = bank[0:2], bank[2:4], bank[4:8]

        w = sb("w", [P, RING, C, D])
        x_sb = sb("x_sb", [P, D])
        xn = sb("xn", [P, D])
        res = sb("res", [P, D])
        a_sb = sb("a_sb", [P, D])
        x1 = sb("x1", [P, D])
        xT = sb("xT", [P, C, P])
        nT = sb("nT", [P, C, P])
        q_sb = sb("q_sb", [P, D])
        k_sb = sb("k_sb", [P, D])
        v_sb = sb("v_sb", [P, D])
        qT = sb("qT", [P, C, P])
        kT = sb("kT", [P, C, P])
        masked = sb("masked", [P, HEADS, P])
        prob = sb("prob", [P, HEADS, P])
        probT = sb("probT", [P, HEADS, P])
        o_sb = sb("o_sb", [P, D])
        up = sb("up", [P, 2, D])
        upT = sb("upT", [P, FF // P, P])
        h_sb = sb("h_sb", [P, D])
        row_sb = sb("row_sb", [P, len(ROWS), D])
        bias_sb = sb("bias_sb", [1, len(BIAS) * D])
        col_sb = sb("col_sb", [P, NCOL])
        edge_i = sb("edge_i", [P, 2 * EC], I32)
        edge_f = sb("edge_f", [P, 2 * EC])
        hot_src = sb("hot_src", [P, EC, P], BF16)
        hot_dst = sb("hot_dst", [P, EC, P], BF16)
        ident = sb("ident", [P, P])
        iota = sb("iota", [P, P])
        ones = sb("ones", [P, P])
        count = sb("count", [P, P])
        count_i = sb("count_i", [P, P])
        mask = sb("mask", [P, P])
        deg = sb("deg", [P, P + 1])
        rdeg = sb("rdeg", [P, P])
        dinv = sb("dinv", [P, P + 1])
        mean_adj = sb("mean_adj", [P, P])
        gcn_adj = sb("gcn_adj", [P, P])
        gin_adj = sb("gin_adj", [P, GIN, P])
        eps1 = sb("eps1", [P, GIN])
        minus_half = sb("minus_half", [P, P + 1])
        stat = sb("stat", [P, 7, 2, 6])
        mv = sb("mv", [P, 7, 2])
        var = sb("var", [P, 7])
        rstd = sb("rstd", [P, 7])
        neg_max = sb("neg_max", [P, HEADS])
        sums = sb("sums", [P, HEADS])
        rsum = sb("rsum", [P, HEADS])
        lsm = sb("lsm", [P, 5])

        x_in = sem("x_in")
        edges_in = sem("edges_in")
        cols_in = sem("cols_in")
        rows_in = sem("rows_in")
        late_rows_in = sem("late_rows_in")
        bias_in = sem("bias_in")
        eps_in = sem("eps_in")
        w_in = {(g, p): sem(f"w_in_{g}{p}") for g in GROUPS for p in range(PIECES.get(g, 1))}
        out_done = sem("out_done")
        pool_step = sem("pool_step")
        ident_ready = sem("ident_ready")
        iota_ready = sem("iota_ready")
        ones_ready = sem("ones_ready")
        edges_ready = sem("edges_ready")
        src_ready = sem("src_ready")
        dst_ready = sem("dst_ready")
        count_full = sem("count_full")
        count_ready = sem("count_ready")
        deg_full = sem("deg_full")
        deg_ready = sem("deg_ready")
        rdeg_ready = sem("rdeg_ready")
        mean_ready = sem("mean_ready")
        gin_adj_ready = sem("gin_adj_ready")
        gcn_adj_ready = sem("gcn_adj_ready")
        dve_step = sem("dve_step")
        var_ready = sem("var_ready")
        rstd_ready = sem("rstd_ready")
        normed = sem("normed")
        turned_full = [sem(f"turned_full{h}") for h in range(2)]
        turned_out = [sem(f"turned_out{h}") for h in range(2)]
        rows_full = [sem(f"rows_full{h}") for h in range(2)]
        rows_out = [sem(f"rows_out{h}") for h in range(2)]
        neigh_full = sem("neigh_full")
        neigh_out = [sem(f"neigh_out{h}") for h in range(2)]
        proj_full = sem("proj_full")
        q_rows = sem("q_rows")
        k_rows = sem("k_rows")
        v_ready = sem("v_ready")
        scores_full = sem("scores_full")
        masked_ready = sem("masked_ready")
        prob_ready = sem("prob_ready")
        probT_full = sem("probT_full")
        probT_ready = sem("probT_ready")
        o_full = sem("o_full")
        o_ready = sem("o_ready")
        up_full = sem("up_full")
        up_rows = sem("up_rows")
        res_ready = sem("res_ready")
        max_ready = sem("max_ready")
        lse_ready = sem("lse_ready")

        def wt(name):
            return w[:, G[name] % RING]

        def col(name, c):
            return col_sb[:, COL[name] + c:COL[name] + c + 1]

        def row(name, h=None):
            i = ROW[name]
            return row_sb[:, i, :] if h is None else row_sb[:, i, h * HALF:(h + 1) * HALF]

        def half(t, h):
            return t[:, h * HALF:(h + 1) * HALF]

        def chunk(t, c):
            return t[:, c * P:(c + 1) * P]

        group_used = {"q": (proj_full, 1), "k": (proj_full, 2), "v": (proj_full, 3), "out": (rows_full[1], R_OUT),
                      **{f"up{j}": (up_full, j + 1) for j in range(4)},
                      **{f"down{j}": (rows_full[1], R_DOWN) for j in range(4)}}

        block = ctx.enter_context(nc.Block())

        @block.sync
        def _(sp):
            sp.dma_start(x_sb[:, :], x).then_inc(x_in, 16)
            for i, name in enumerate(GROUPS):
                if i >= RING:
                    sp.wait_ge(*group_used[GROUPS[i - RING]])
                n = PIECES.get(name, 1)
                for p in range(n):
                    cs = slice(p * C // n, (p + 1) * C // n)
                    sp.dma_start(wt(name)[:, cs, :], weights[i, :, cs, :]).then_inc(w_in[(name, p)], 16)
            for h in range(2):
                sp.wait_ge(normed, 2 * 5 + h + 1)
                sp.dma_start(half(out, h), half(res, h)).then_inc(out_done, 16)
            sp.wait_ge(out_done, 32)

        @block.gpsimd
        def _(pool):
            done = [0]

            def link(ins):
                done[0] += 1
                ins.then_inc(pool_step, 1)
                pool.wait_ge(pool_step, done[0])

            def rsqrt_of_variance(i):
                pool.wait_ge(var_ready, i + 1)
                pool.tensor_tensor(rstd[:, i:i + 1], var[:, i:i + 1], minus_half[:, 0:1], ALU.pow)\
                    .then_inc(rstd_ready, 1)

            link(pool.memset(minus_half[:, :], -0.5))
            link(pool.memset(ident[:, :], 0.0))
            pool.affine_select(out=ident[:, :], in_=ident[:, :], compare_op=ALU.not_equal, fill=1.0, base=0,
                               pattern=[[-1, P]], channel_multiplier=1).then_inc(ident_ready, 1)
            pool.iota(iota[:, :], pattern=[[1, P]], base=0, channel_multiplier=0,
                      allow_small_or_imprecise_dtypes=True).then_inc(iota_ready, 1)
            pool.memset(ones[:, :], 1.0).then_inc(ones_ready, 1)
            rsqrt_of_variance(LN1)
            pool.wait_ge(iota_ready, 1)
            pool.wait_ge(edges_ready, 1)
            for e in range(EC):
                ins = pool.tensor_scalar(hot_dst[:, e, :], iota[:, :], edge_f[:, EC + e:EC + e + 1], None, ALU.is_equal)
            ins.then_inc(dst_ready, 1)
            pool.wait_ge(x_in, 16)
            pool.wait_ge(rows_in, 16)
            pool.tensor_tensor(res[:, :], x_sb[:, :], row("b_out"), ALU.add).then_inc(res_ready, 1)
            pool.wait_ge(eps_in, 16)
            link(pool.tensor_scalar(eps1[:, :], eps1[:, :], 1.0, None, ALU.add))
            pool.wait_ge(ident_ready, 1)
            for i in range(GIN):
                link(pool.tensor_scalar(gin_adj[:, i, :], ident[:, :], eps1[:, i:i + 1], None, ALU.mult))
            pool.wait_ge(count_ready, 1)
            pool.tensor_tensor(gin_adj[:, :, :], gin_adj[:, :, :],
                               count[:, :].unsqueeze(1).broadcast_to([P, GIN, P]), ALU.add)\
                .then_inc(gin_adj_ready, 1)
            pool.wait_ge(deg_ready, 1)
            link(pool.tensor_scalar(dinv[:, :], deg[:, :], 1.0, None, ALU.add))
            link(pool.tensor_tensor(dinv[:, :], dinv[:, :], minus_half[:, :], ALU.pow))
            link(pool.tensor_scalar(gcn_adj[:, :], count_i[:, :], dinv[:, P:P + 1], None, ALU.mult))
            pool.tensor_tensor(gcn_adj[:, :], gcn_adj[:, :], dinv[:, 0:P], ALU.mult).then_inc(gcn_adj_ready, 1)
            rsqrt_of_variance(LN2)
            pool.wait_ge(late_rows_in, 16)
            link(pool.tensor_tensor(res[:, :], x_sb[:, :], row("b_down"), ALU.add))
            for h in range(2):
                pool.wait_ge(rows_out[h], R_OUT)
            pool.tensor_tensor(res[:, :], res[:, :], a_sb[:, :], ALU.add).then_inc(res_ready, 1)
            pool.wait_ge(rdeg_ready, 1)
            pool.tensor_tensor(mean_adj[:, :], count[:, :], rdeg[:, :], ALU.mult).then_inc(mean_ready, 1)
            rsqrt_of_variance(LNX1)
            pool.wait_ge(normed, 2 * 2 + 2)
            pool.tensor_tensor(res[:, :], x1[:, :], row("beta"), ALU.add).then_inc(res_ready, 1)
            rsqrt_of_variance(LNH)
            rsqrt_of_variance(LNX2)
            rsqrt_of_variance(LNX3)
            pool.wait_ge(normed, 2 * 4 + 2)
            pool.tensor_tensor(res[:, :], xn[:, :], row("b_dense"), ALU.add).then_inc(res_ready, 1)
            rsqrt_of_variance(LNX4)

        @block.scalar
        def _(act):
            act.dma_start(edge_i[:, :], edges).then_inc(edges_in, 16)
            act.dma_start(col_sb[:, :], cols).then_inc(cols_in, 16)
            act.dma_start(row_sb[:, 0:2, :], rows[0:2, :].partition_broadcast(P)).then_inc(rows_in, 16)
            act.dma_start(eps1[:, :], eps.partition_broadcast(P)).then_inc(eps_in, 16)
            act.dma_start(bias_sb[:, :], bias_rows).then_inc(bias_in, 16)
            act.dma_start(row_sb[:, 2:, :], rows[2:, :].partition_broadcast(P)).then_inc(late_rows_in, 16)

            def empty_turned(n, dst, scale=None, bias=None, func=ACT.Identity):
                act.wait_ge(turned_full[0], n)
                if bias is None:
                    act.activation(dst, T[0][:, 0:HALF].rearrange("p (c n) -> p c n", c=2), ACT.Copy)\
                        .then_inc(turned_out[0], 1)
                    return
                for c in range(2):
                    ins = act.activation(dst[:, c, :], chunk(T[0], c), func, bias=bias(c),
                                         scale=1.0 if scale is None else scale(c))
                ins.then_inc(turned_out[0], 1)

            act.wait_ge(cols_in, 16)
            empty_turned(T_LN1, xT[:, 0:2, :], lambda c: col("ln1_w", c), lambda c: col("ln1_b", c))
            act.wait_ge(proj_full, 1)
            act.activation(q_sb[:, :], U[0][:, :], ACT.Copy).then_inc(q_rows, 1)
            empty_turned(T_Q, qT[:, 0:2, :], None, lambda c: col("b_q", c))
            empty_turned(T_K, kT[:, 0:2, :], None, lambda c: col("b_k", c))
            for i, h in enumerate(HEAD_ORDER):
                act.wait_ge(masked_ready, i + 1)
                act.activation(prob[:, h, :], masked[:, h, :], ACT.Exp, bias=neg_max[:, h:h + 1], scale=-1.0,
                               accum_out=sums[:, h:h + 1]).then_inc(prob_ready, 1)
            empty_turned(T_O, xT[:, 0:2, :])
            empty_turned(T_LN2, xT[:, 0:2, :], lambda c: col("ln2_w", c), lambda c: col("ln2_b", c))

            def up_to_sbuf(j):
                act.wait_ge(up_full, j + 1)
                if j >= 2:
                    act.wait_ge(turned_full[1], T_UP + j - 2)
                act.activation(up[:, j % 2, :], U[j][:, :], ACT.Copy).then_inc(up_rows, 1)

            def up_turned(j):
                empty_turned(T_UP + j, upT[:, C * j:C * j + 2, :], None, lambda c: col("b_up", C * j + c), ACT.Relu)

            up_to_sbuf(0)
            up_to_sbuf(1)
            up_turned(0)
            up_to_sbuf(2)
            up_turned(1)
            up_to_sbuf(3)
            up_turned(2)
            up_turned(3)
            empty_turned(T_X1, xT[:, 0:2, :])
            act.wait_ge(neigh_full, 1)
            act.activation(nT[:, 0:2, :], U[0][:, 0:HALF].rearrange("p (c n) -> p c n", c=2), ACT.Copy)\
                .then_inc(neigh_out[0], 1)
            for i in range(GIN):
                empty_turned(T_GIN + i, xT[:, 0:2, :])
                act.wait_ge(rows_full[0], R_GIN + i)
                act.activation(half(h_sb, 0), R[0][:, 0:HALF], ACT.Relu).then_inc(rows_out[0], 1)
            act.wait_ge(max_ready, 1)
            act.activation(a_sb[:, :], h_sb[:, :], ACT.Exp, bias=lsm[:, 1:2], accum_out=lsm[:, 2:3])\
                .then_inc(lse_ready, 1)
            act.wait_ge(lse_ready, 1)
            act.activation(lsm[:, 3:4], lsm[:, 2:3], ACT.Ln).then_inc(lse_ready, 1)
            empty_turned(T_X3, xT[:, 0:2, :])
            act.wait_ge(rows_full[0], R_GCN)
            act.activation(half(h_sb, 0), R[0][:, 0:HALF], ACT.Copy).then_inc(rows_out[0], 1)
            empty_turned(T_AGG, xT[:, 0:2, :], None, lambda c: col("b_gcn", c))

        @block.tensor
        def _(pe):
            def turn(n, src, ready, first):
                for h in range(2):
                    pe.wait_ge(ready, first + h)
                    if n > 1:
                        pe.wait_ge(turned_out[h], n - 1)
                    for c in range(2):
                        ins = pe.transpose(chunk(T[h], c), chunk(src, 2 * h + c), ident[:, :])
                    ins.then_inc(turned_full[h], 1)

            def aggregate(n, src, adj, ready, first):
                for h in range(2):
                    pe.wait_ge(ready[h], first[h])
                    pe.wait_ge(turned_out[h], n - 1)
                    for c in range(2):
                        ins = pe.matmul(chunk(T[h], c), chunk(src, 2 * h + c), adj, start=True, stop=True)
                    ins.then_inc(turned_full[h], 1)

            def bias_row(name, r, h):
                pe.wait_ge(bias_in, 16)
                pe.wait_ge(rows_out[h], r - 1)
                i = BIAS.index(name)
                pe.matmul(R[h][:, 0:HALF], ones[0:1, :], bias_sb[0:1, i * D + h * HALF:i * D + (h + 1) * HALF],
                          start=True, stop=False)

            def product(r, n, g, lhs, bias=None, last=True):
                pe.wait_ge(w_in[(g, 0)], 16)
                for h in range(2):
                    if bias is None:
                        if r > 1:
                            pe.wait_ge(rows_out[h], r - 1)
                    else:
                        bias_row(bias, r, h)
                    for c in range(C):
                        if h == 0 and c % 2 == 0:
                            pe.wait_ge(turned_out[c // 2], n)
                        ins = pe.matmul(R[h][:, 0:HALF], lhs[:, c, :], half(wt(g)[:, c, :], h),
                                        start=(bias is None and c == 0), stop=(last and c == C - 1))
                    if last:
                        ins.then_inc(rows_full[h], 1)

            def project(i, g, cs):
                n = PIECES[g]
                for c in cs:
                    pe.wait_ge(w_in[(g, c * n // C)], 16)
                    if i == 0 and c % 2 == 0:
                        pe.wait_ge(turned_out[c // 2], T_LN1)
                    ins = pe.matmul(U[i][:, :], xT[:, c, :], wt(g)[:, c, :], start=(c == 0), stop=(c == C - 1))
                if cs[-1] == C - 1:
                    ins.then_inc(proj_full, 1)

            pe.wait_ge(ident_ready, 1)
            turn(T_LN1, xn, normed, 1)
            project(0, "q", range(C))
            project(1, "k", range(C))
            pe.wait_ge(src_ready, 1)
            pe.wait_ge(dst_ready, 1)
            for e in range(EC):
                ins = pe.matmul(U[3][:, 0:P], hot_src[:, e, :], hot_dst[:, e, :], start=(e == 0), stop=(e == EC - 1))
            ins.then_inc(count_full, 1)

            def turn_rows(n, src, ready):
                pe.wait_ge(ready, 1)
                for h in range(2):
                    pe.wait_ge(turned_out[h], n - 1)
                    for c in range(2):
                        ins = pe.transpose(chunk(T[h], c), chunk(src, 2 * h + c), ident[:, :])
                    ins.then_inc(turned_full[h], 1)

            turn_rows(T_Q, q_sb, q_rows)
            project(2, "v", range(0, 2))
            pe.wait_ge(count_ready, 1)
            pe.wait_ge(ones_ready, 1)
            pe.matmul(U[3][:, 0:P], ones[:, :], count[:, :], start=True, stop=True)
            pe.matmul(U[3][:, P:P + 1], count[:, :], ones[:, 0:1], start=True, stop=True).then_inc(deg_full, 1)
            turn_rows(T_K, k_sb, k_rows)
            project(2, "v", range(2, C))

            score_bank = [R[0], R[1], U[0], U[1]]
            for h in range(HEADS):
                if h % 4 == 0:
                    pe.wait_ge(turned_out[h // 4], T_K)
                lo = (h % 2) * DH
                b = score_bank[2 * (h // 4) + h % 2]
                at = (h % 4) // 2
                ins = pe.matmul(b[:, at * P:(at + 1) * P], qT[lo:lo + DH, h // 2, :], kT[lo:lo + DH, h // 2, :],
                                start=True, stop=True)
                if h % 4 >= 2:
                    ins.then_inc(scores_full, 1)

            prob_bank = [U[3], U[2], R[0], R[1]]

            def turn_prob(i):
                if i == 0:
                    pe.wait_ge(deg_ready, 1)
                if i == 1:
                    pe.wait_ge(v_ready, 1)
                pe.wait_ge(prob_ready, 2 * i + 2)
                for k in range(2):
                    ins = pe.transpose(chunk(prob_bank[i], k), prob[:, HEAD_ORDER[2 * i + k], :], ident[:, :])
                ins.then_inc(probT_full, 1)

            def attend(i):
                pe.wait_ge(probT_ready, i + 1)
                for h in HEAD_ORDER[2 * i:2 * i + 2]:
                    ins = pe.matmul(U[h // 4][:, (h % 4) * DH:(h % 4 + 1) * DH], probT[:, h, :],
                                    v_sb[:, h * DH:(h + 1) * DH], start=True, stop=True)
                if i % 2:
                    ins.then_inc(o_full, 1)

            turn_prob(0)
            turn_prob(1)
            turn_prob(2)
            attend(0)
            attend(1)
            turn_prob(3)
            attend(2)
            attend(3)
            turn(T_O, o_sb, o_ready, 1)
            product(R_OUT, T_O, "out", xT)
            turn(T_LN2, xn, normed, 3)

            def up_block(j):
                pe.wait_ge(w_in[(f"up{j}", 0)], 16)
                for c in range(C):
                    if j == 0 and c % 2 == 0:
                        pe.wait_ge(turned_out[c // 2], T_LN2)
                    ins = pe.matmul(U[j][:, :], xT[:, c, :], wt(f"up{j}")[:, c, :], start=(c == 0), stop=(c == C - 1))
                ins.then_inc(up_full, 1)

            def turn_up(j):
                pe.wait_ge(up_rows, j + 1)
                for h in range(2):
                    pe.wait_ge(turned_out[h], T_UP + j - 1)
                    for c in range(2):
                        ins = pe.transpose(chunk(T[h], c), up[:, j % 2, (2 * h + c) * P:(2 * h + c + 1) * P], ident[:, :])
                    ins.then_inc(turned_full[h], 1)

            def down_block(j, halves):
                pe.wait_ge(w_in[(f"down{j}", 0)], 16)
                for h in halves:
                    for c in range(C):
                        pe.wait_ge(turned_out[c // 2], T_UP + j)
                        ins = pe.matmul(R[h][:, 0:HALF], upT[:, C * j + c, :], half(wt(f"down{j}")[:, c, :], h),
                                        start=(j == 0 and c == 0), stop=(j == 3 and c == C - 1))
                    if j == 3:
                        ins.then_inc(rows_full[h], 1)

            up_block(0)
            up_block(1)
            turn_up(0)
            up_block(2)
            turn_up(1)
            up_block(3)
            turn_up(2)
            for h in range(2):
                pe.wait_ge(rows_out[h], R_DOWN - 1)
            down_block(0, range(2))
            turn_up(3)
            down_block(1, range(2))
            down_block(2, range(2))
            down_block(3, range(2))

            turn(T_X1, x1, normed, 5)
            pe.wait_ge(mean_ready, 1)
            for h in range(2):
                for c in range(2):
                    ins = pe.matmul(chunk(U[h], c), chunk(x1, 2 * h + c), mean_adj[:, :], start=True, stop=True)
                ins.then_inc(neigh_full, 1)
            product(R_L1, T_X1, "self", xT, bias="l1", last=False)
            pe.wait_ge(w_in[("neigh", 0)], 16)
            for h in range(2):
                for c in range(C):
                    if h == 0 and c % 2 == 0:
                        pe.wait_ge(neigh_out[c // 2], 1)
                    ins = pe.matmul(R[h][:, 0:HALF], nT[:, c, :], half(wt("neigh")[:, c, :], h),
                                    start=False, stop=(c == C - 1))
                ins.then_inc(rows_full[h], 1)

            pe.wait_ge(gin_adj_ready, 1)
            for i in range(GIN):
                if i == 0:
                    aggregate(T_GIN, xn, gin_adj[:, 0, :], [normed, normed], [7, 8])
                else:
                    aggregate(T_GIN + i, h_sb, gin_adj[:, i, :], rows_out, [R_GIN + i - 1] * 2)
                product(R_GIN + i, T_GIN + i, f"gin{i}", xT, bias=f"gin{i}")

            turn(T_X3, xn, normed, 9)
            product(R_GCN, T_X3, "gcn", xT)
            pe.wait_ge(gcn_adj_ready, 1)
            aggregate(T_AGG, h_sb, gcn_adj[:, :], rows_out, [R_GCN] * 2)
            product(R_DENSE, T_AGG, "dense", xT)

        @block.vector
        def _(dve):
            done = [0]

            def mark(ins):
                done[0] += 1
                ins.then_inc(dve_step, 1)

            def link(ins):
                mark(ins)
                dve.wait_ge(dve_step, done[0])

            def stats(i, h, src):
                mark(dve.bn_stats(stat[:, i, h, :], src))

            def mean_and_rstd(i):
                dve.wait_ge(dve_step, done[0])
                link(dve.bn_aggr(mv[:, i, :], stat[:, i, :, :].rearrange("p a b -> p (a b)")))
                dve.tensor_scalar(var[:, i:i + 1], mv[:, i, 1:2], LN_EPS, None, ALU.add).then_inc(var_ready, 1)
                dve.wait_ge(rstd_ready, i + 1)

            def apply(i, src, dst):
                for h in range(2):
                    dve.tensor_scalar(half(dst, h), half(src, h), mv[:, i, 0:1], rstd[:, i:i + 1],
                                      ALU.subtract, ALU.mult).then_inc(normed, 1)

            def empty_turned(n, dst, scale=None, bias=None, relu=False):
                dve.wait_ge(turned_full[1], n)
                if bias is None:
                    dve.tensor_copy(dst, T[1][:, 0:HALF].rearrange("p (c n) -> p c n", c=2))\
                        .then_inc(turned_out[1], 1)
                    return
                for c in range(2):
                    if scale is not None:
                        ins = dve.tensor_scalar(dst[:, c, :], chunk(T[1], c), scale(2 + c), bias(2 + c),
                                                ALU.mult, ALU.add)
                    elif relu:
                        ins = dve.tensor_scalar(dst[:, c, :], chunk(T[1], c), bias(2 + c), 0.0, ALU.add, ALU.max)
                    else:
                        ins = dve.tensor_scalar(dst[:, c, :], chunk(T[1], c), bias(2 + c), None, ALU.add)
                ins.then_inc(turned_out[1], 1)

            dve.wait_ge(x_in, 16)
            for h in range(2):
                stats(LN1, h, half(x_sb, h))
            mean_and_rstd(LN1)
            apply(LN1, x_sb, xn)
            dve.wait_ge(edges_in, 16)
            dve.tensor_copy(edge_f[:, :], edge_i[:, :]).then_inc(edges_ready, 1)
            dve.wait_ge(cols_in, 16)
            empty_turned(T_LN1, xT[:, 2:4, :], lambda c: col("ln1_w", c), lambda c: col("ln1_b", c))
            dve.wait_ge(edges_ready, 1)
            dve.wait_ge(iota_ready, 1)
            for e in range(EC):
                ins = dve.tensor_scalar(hot_src[:, e, :], iota[:, :], edge_f[:, e:e + 1], None, ALU.is_equal)
            ins.then_inc(src_ready, 1)
            dve.wait_ge(proj_full, 2)
            dve.tensor_copy(k_sb[:, :], U[1][:, :]).then_inc(k_rows, 1)
            dve.wait_ge(count_full, 1)
            dve.wait_ge(ident_ready, 1)
            mark(dve.tensor_tensor(count_i[:, :], U[3][:, 0:P], ident[:, :], ALU.add))
            dve.tensor_copy(count[:, :], U[3][:, 0:P]).then_inc(count_ready, 1)
            empty_turned(T_Q, qT[:, 2:4, :], None, lambda c: col("b_q", c))
            dve.wait_ge(dve_step, done[0])
            link(dve.tensor_scalar(mask[:, :], count_i[:, :], 0.0, NEG, ALU.is_equal, ALU.mult))
            dve.wait_ge(deg_full, 1)
            dve.tensor_copy(deg[:, :], U[3][:, 0:P + 1]).then_inc(deg_ready, 1)
            empty_turned(T_K, kT[:, 2:4, :], None, lambda c: col("b_k", c))
            dve.wait_ge(proj_full, 3)
            dve.wait_ge(rows_in, 16)
            dve.tensor_tensor(v_sb[:, :], U[2][:, :], row("b_v"), ALU.add).then_inc(v_ready, 1)
            score_bank = [R[0], R[1], U[0], U[1]]
            for i in range(4):
                dve.wait_ge(scores_full, i + 1)
                for k in range(2):
                    h = HEAD_ORDER[2 * i + k]
                    link(dve.scalar_tensor_tensor(masked[:, h, :], chunk(score_bank[i], k), -(DH ** -0.5),
                                                  mask[:, :], ALU.mult, ALU.add))
                    dve.tensor_reduce(neg_max[:, h:h + 1], masked[:, h, :], AX_X, ALU.min)\
                        .then_inc(masked_ready, 1)
            prob_bank = [U[3], U[2], R[0], R[1]]

            def probT_to_sbuf(i):
                dve.wait_ge(probT_full, i + 1)
                for k in range(2):
                    ins = dve.tensor_copy(probT[:, HEAD_ORDER[2 * i + k], :], chunk(prob_bank[i], k))
                ins.then_inc(probT_ready, 1)

            def normalise_o(g):
                dve.wait_ge(prob_ready, 4 * g + 4)
                link(dve.reciprocal(rsum[:, 4 * g:4 * g + 4], sums[:, 4 * g:4 * g + 4]))
                dve.wait_ge(o_full, g + 1)
                dve.tensor_tensor(half(o_sb, g).rearrange("p (h d) -> p h d", h=4),
                                  U[g][:, 0:HALF].rearrange("p (h d) -> p h d", h=4),
                                  rsum[:, 4 * g:4 * g + 4].unsqueeze(2).broadcast_to([P, 4, DH]),
                                  ALU.mult).then_inc(o_ready, 1)

            probT_to_sbuf(0)
            probT_to_sbuf(1)
            probT_to_sbuf(2)
            normalise_o(0)
            probT_to_sbuf(3)
            normalise_o(1)
            empty_turned(T_O, xT[:, 2:4, :])
            dve.wait_ge(res_ready, 1)
            for h in range(2):
                dve.wait_ge(rows_full[h], R_OUT)
                dve.tensor_tensor(half(a_sb, h), R[h][:, 0:HALF], half(res, h), ALU.add).then_inc(rows_out[h], 1)
                dve.wait_ge(rows_out[h], R_OUT)
                stats(LN2, h, half(a_sb, h))
            mean_and_rstd(LN2)
            apply(LN2, a_sb, xn)
            empty_turned(T_LN2, xT[:, 2:4, :], lambda c: col("ln2_w", c), lambda c: col("ln2_b", c))
            link(dve.tensor_scalar(rdeg[:, :], deg[:, 0:P], 1.0, None, ALU.max))
            dve.reciprocal(rdeg[:, :], rdeg[:, :]).then_inc(rdeg_ready, 1)
            for j in range(4):
                empty_turned(T_UP + j, upT[:, C * j + 2:C * j + 4, :], None, lambda c: col("b_up", C * j + c), relu=True)
            dve.wait_ge(res_ready, 2)
            for h in range(2):
                dve.wait_ge(rows_full[h], R_DOWN)
                dve.tensor_tensor(half(x1, h), R[h][:, 0:HALF], half(res, h), ALU.add).then_inc(rows_out[h], 1)
                dve.wait_ge(rows_out[h], R_DOWN)
                stats(LNX1, h, half(x1, h))
            mean_and_rstd(LNX1)
            apply(LNX1, x1, x1)
            empty_turned(T_X1, xT[:, 2:4, :])
            dve.wait_ge(neigh_full, 2)
            dve.tensor_copy(nT[:, 2:4, :], U[1][:, 0:HALF].rearrange("p (c n) -> p c n", c=2))\
                .then_inc(neigh_out[1], 1)
            for h in range(2):
                dve.wait_ge(rows_full[h], R_L1)
                stats(LNH, h, R[h][:, 0:HALF])
            mean_and_rstd(LNH)
            dve.wait_ge(res_ready, 3)
            for h in range(2):
                dve.scalar_tensor_tensor(half(xn, h), R[h][:, 0:HALF], mv[:, LNH, 0:1], row("gamma", h),
                                         ALU.subtract, ALU.mult).then_inc(rows_out[h], 1)
            for h in range(2):
                dve.wait_ge(rows_out[h], R_L1)
                link(dve.scalar_tensor_tensor(half(xn, h), half(xn, h), rstd[:, LNH:LNH + 1], half(res, h),
                                              ALU.mult, ALU.add))
                stats(LNX2, h, half(xn, h))
            mean_and_rstd(LNX2)
            apply(LNX2, xn, xn)
            for i in range(GIN):
                empty_turned(T_GIN + i, xT[:, 2:4, :])
                dve.wait_ge(rows_full[1], R_GIN + i)
                dve.tensor_scalar(half(h_sb, 1), R[1][:, 0:HALF], 0.0, None, ALU.max).then_inc(rows_out[1], 1)
            for h in range(2):
                dve.wait_ge(rows_out[h], R_GIN + GIN - 1)
            link(dve.tensor_reduce(lsm[:, 0:1], h_sb[:, :], AX_X, ALU.max))
            dve.tensor_scalar(lsm[:, 1:2], lsm[:, 0:1], -1.0, None, ALU.mult).then_inc(max_ready, 1)
            dve.wait_ge(lse_ready, 2)
            link(dve.tensor_tensor(lsm[:, 4:5], lsm[:, 0:1], lsm[:, 3:4], ALU.add))
            for h in range(2):
                link(dve.scalar_tensor_tensor(half(xn, h), half(h_sb, h), lsm[:, 4:5], half(xn, h),
                                              ALU.subtract, ALU.add))
                stats(LNX3, h, half(xn, h))
            mean_and_rstd(LNX3)
            apply(LNX3, xn, xn)
            empty_turned(T_X3, xT[:, 2:4, :])
            dve.wait_ge(rows_full[1], R_GCN)
            dve.tensor_copy(half(h_sb, 1), R[1][:, 0:HALF]).then_inc(rows_out[1], 1)
            empty_turned(T_AGG, xT[:, 2:4, :], None, lambda c: col("b_gcn", c))
            dve.wait_ge(res_ready, 4)
            for h in range(2):
                dve.wait_ge(rows_full[h], R_DENSE)
                link(dve.tensor_tensor(half(res, h), R[h][:, 0:HALF], half(res, h), ALU.add))
                stats(LNX4, h, half(res, h))
            mean_and_rstd(LNX4)
            apply(LNX4, res, res)


def kernel(**inputs):
    import numpy as np
    import concourse.bacc as bacc
    from concourse.bass_utils import run_bass_kernel_spmd as run

    a = {k: np.asarray(v) for k, v in inputs.items()}
    w_in, w1, w2 = a["L0_gnn_w_in"], a["L0_gnn_w1"], a["L0_gnn_w2"]
    by_name = {"q": w_in[0:D].T, "k": w_in[D:2 * D].T, "v": w_in[2 * D:3 * D].T, "out": a["L0_gnn_w_out"].T,
               "self": a["L1_gnn_W_self"].T, "neigh": a["L1_gnn_W_neigh"].T, "gin0": a["L2_gnn_W1"],
               "gcn": a["L3_gnn_W_gcn"], "dense": a["L3_gnn_W_dense"]}
    for j in range(4):
        by_name[f"up{j}"] = w1[j * D:(j + 1) * D].T
        by_name[f"down{j}"] = w2.T[j * D:(j + 1) * D]
        by_name[f"gin{j + 1}"] = a["L2_gnn_Ws"][j]
    weights = np.stack([by_name[g].reshape(C, P, D).transpose(1, 0, 2) for g in GROUPS])
    b_in = a["L0_gnn_b_in"]
    columns = {"ln1_w": a["L0_gnn_ln1_w"], "ln1_b": a["L0_gnn_ln1_b"], "b_q": b_in[0:D], "b_k": b_in[D:2 * D],
               "ln2_w": a["L0_gnn_ln2_w"], "ln2_b": a["L0_gnn_ln2_b"], "b_up": a["L0_gnn_b1"],
               "b_gcn": a["L3_gnn_b_gcn"]}
    cols = np.concatenate([columns[name].reshape(-1, P).T for name, _ in COLS], axis=1)
    all_rows = {"b_v": b_in[2 * D:3 * D], "b_out": a["L0_gnn_b_out"], "b_down": a["L0_gnn_b2"],
                "gamma": a["L1_gnn_gamma"], "beta": a["L1_gnn_beta"], "b_dense": a["L3_gnn_b_dense"]}
    rows = np.stack([all_rows[name] for name in ROWS])
    bias_rows = np.concatenate([a["L1_gnn_bias"], a["L2_gnn_b1"], a["L2_gnn_bs"].reshape(-1)]).reshape(1, -1)
    edges = np.concatenate([a["src"].reshape(P, EC), a["dst"].reshape(P, EC)], axis=1)
    arrays = {"x": a["x"], "edges": edges, "cols": cols, "rows": rows, "bias_rows": bias_rows,
              "eps": a["L2_gnn_eps"], "weights": weights}
    arrays = {f"in_{k}": np.ascontiguousarray(v) for k, v in arrays.items()}

    nc = bacc.Bacc("TRN2", target_bir_lowering=False, num_devices=1)
    args = [nc.dram_tensor(k, v.shape, mybir.dt.from_np(v.dtype), kind="ExternalInput").ap()
            for k, v in arrays.items()]
    result = nc.dram_tensor("out_x", (P, D), F32, kind="ExternalOutput").ap()
    residual_gnn(nc, *args, result)
    got = run(nc, [arrays], core_ids=[0])
    return got.results[0]["out_x"]
```

```python
from contextlib import ExitStack

import concourse.bass as bass
from concourse import mybir

ALU = mybir.AluOpType
ACT = mybir.ActivationFunctionType
F32 = mybir.dt.float32
F32R = mybir.dt.float32r
BF16 = mybir.dt.bfloat16
I32 = mybir.dt.int32
AX_X = mybir.AxisListType.X

P = 128
D = 512
C = D // P
HALF = D // 2
HEADS = 8
DH = D // HEADS
FF = 4 * D
EDGES = 2 * 1024 + P
EC = EDGES // P
GIN = 5
LN_EPS = 1e-5
NEG = 1e9
WARM = {"start": 10, "ln2": 10, "x1": 8, "x2": 18, "x3": 11}
RAW_RING = 4
SPLIT_RING = 5

GROUPS = (["q", "k", "v", "out"] + [f"up{j}" for j in range(4)] + [f"down{j}" for j in range(4)]
          + ["self", "neigh"] + [f"gin{i}" for i in range(GIN)] + ["gcn", "dense"])
G = {name: i for i, name in enumerate(GROUPS)}
PIECES = {"q": 4, "k": 2, "v": 2, "out": 2}

COLS = [("ln1_w", C), ("ln1_b", C), ("b_q", C), ("b_k", C), ("ln2_w", C), ("ln2_b", C), ("b_up", FF // P), ("b_gcn", C)]
COL = {}
for _name, _n in COLS:
    COL[_name] = sum(n for m, n in COLS[:[m for m, _ in COLS].index(_name)])
NCOL = sum(n for _, n in COLS)
ROWS = ["b_v", "b_out", "b_down", "gamma", "beta", "b_dense"]
ROW = {name: i for i, name in enumerate(ROWS)}
BK = 64
BIAS = ["l1"] + [f"gin{i}" for i in range(GIN)]

LO_ON_POOL = {name: (0, 1) for name in GROUPS}


def lo_count(name, on_pool, upto=C):
    return sum((k in LO_ON_POOL[g]) == on_pool for g in GROUPS[:G[name] + 1]
               for k in range(upto if g == name else C))


HEAD_ORDER = [0, 2, 1, 3, 4, 6, 5, 7]

LN1, LN2, LNX1, LNH, LNX2, LNX3, LNX4 = range(7)
(T_LN1, T_Q, T_K, T_O, T_LN2, T_UP, T_X1, T_GIN, T_X3, T_AGG) = (1, 2, 3, 4, 5, 6, 10, 11, 16, 17)
HI_FILLS = [T_LN1, T_O, T_LN2, T_X1, *range(T_GIN, T_GIN + GIN), T_X3, T_AGG]
(R_OUT, R_DOWN, R_L1, R_GIN, R_GCN, R_DENSE) = (1, 2, 3, 4, 9, 10)


def residual_gnn(nc, x, edges, cols, rows, bias_rows, eps, weights, out):
    with ExitStack() as ctx:
        def sb(name, shape, dt=F32):
            return ctx.enter_context(nc.sbuf_tensor(name, shape, dt))

        def sem(name):
            return ctx.enter_context(nc.semaphore(name))

        bank = [ctx.enter_context(nc.psum_tensor(f"bank{i}", [P, 512], F32)) for i in range(8)]
        T, R, U = bank[0:2], bank[2:4], bank[4:8]

        raw = sb("raw", [P, RAW_RING, C, D])
        w_hi = sb("w_hi", [P, SPLIT_RING, C, D], F32R)
        w_lo = sb("w_lo", [P, SPLIT_RING, C, D], F32R)

        x_sb = sb("x_sb", [P, D])
        xn = sb("xn", [P, D])
        res = sb("res", [P, D])
        a_sb = sb("a_sb", [P, D])
        x1 = sb("x1", [P, D])
        xT_hi = sb("xT_hi", [P, C, P], F32R)
        xT_lo = sb("xT_lo", [P, C, P], F32R)
        xT = sb("xT", [P, C, P])
        row_sb = sb("row_sb", [P, len(ROWS), D])
        bias_hl = sb("bias_hl", [BK, len(BIAS) * D], F32R)
        col_sb = sb("col_sb", [P, NCOL])
        ident = sb("ident", [P, P])
        iota = sb("iota", [P, P])
        ones = sb("ones", [P, P])
        ones_r = sb("ones_r", [BK, P], F32R)
        count = sb("count", [P, P])
        count_i = sb("count_i", [P, P])
        mask = sb("mask", [P, P])
        deg = sb("deg", [P, P + 1])
        rdeg = sb("rdeg", [P, P])
        dinv = sb("dinv", [P, 1])
        dinv_diag = sb("dinv_diag", [P, P])
        dinv_row = sb("dinv_row", [P, P])
        mean_adj = sb("mean_adj", [P, P])
        gcn_adj = sb("gcn_adj", [P, P])
        gin_adj = sb("gin_adj", [P, GIN, P])
        eps1 = sb("eps1", [P, GIN])
        minus_half = sb("minus_half", [P, 1])
        stat = sb("stat", [P, 7, 2, 6])
        mv = sb("mv", [P, 7, 2])
        var = sb("var", [P, 7])
        rstd = sb("rstd", [P, 7])
        neg_max = sb("neg_max", [P, HEADS])
        sums = sb("sums", [P, HEADS])
        rsum = sb("rsum", [P, HEADS])
        lsm = sb("lsm", [P, 5])

        with ExitStack() as attention:
            def tmp(name, shape, dt=F32):
                return attention.enter_context(nc.sbuf_tensor(name, shape, dt))

            edge_i = tmp("edge_i", [P, 2 * EC], I32)
            edge_f = tmp("edge_f", [P, 2 * EC])
            hot_src = tmp("hot_src", [P, EC, P], BF16)
            hot_dst = tmp("hot_dst", [P, EC, P], BF16)
            q_sb = tmp("q_sb", [P, D])
            k_sb = tmp("k_sb", [P, D])
            v_sb = tmp("v_sb", [P, D])
            qT = tmp("qT", [P, C, P])
            kT = tmp("kT", [P, C, P])
            masked = tmp("masked", [P, HEADS, P])
            prob = tmp("prob", [P, HEADS, P])
            probT = tmp("probT", [P, HEADS, P])
            o_sb = tmp("o_sb", [P, D])
            bias_raw = tmp("bias_raw", [BK, len(BIAS) * D])
        up = sb("up", [P, 2, D])
        up_act = sb("up_act", [P, 2, C, P])
        upT_hi = sb("upT_hi", [P, FF // P, P], F32R)
        upT_lo = sb("upT_lo", [P, FF // P, P], F32R)
        nT_hi = sb("nT_hi", [P, C, P], F32R)
        nT_lo = sb("nT_lo", [P, C, P], F32R)
        h_sb = sb("h_sb", [P, D])

        x_in = sem("x_in")
        edges_in = sem("edges_in")
        cols_in = sem("cols_in")
        rows_in = sem("rows_in")
        late_rows_in = sem("late_rows_in")
        bias_in = sem("bias_in")
        eps_in = sem("eps_in")
        w_in = {(g, p): sem(f"w_in_{g}{p}") for g in GROUPS for p in range(PIECES.get(g, 1))}
        out_done = sem("out_done")
        w_hi_ready = sem("w_hi_ready")
        w_lo_pool = sem("w_lo_pool")
        w_lo_dve = sem("w_lo_dve")
        bias_zero = sem("bias_zero")
        bias_hi_ready = sem("bias_hi_ready")
        bias_ready = sem("bias_ready")
        ones_r_ready = sem("ones_r_ready")
        pool_step = sem("pool_step")
        ident_ready = sem("ident_ready")
        iota_ready = sem("iota_ready")
        ones_ready = sem("ones_ready")
        edges_ready = sem("edges_ready")
        src_ready = sem("src_ready")
        dst_ready = sem("dst_ready")
        count_full = sem("count_full")
        count_ready = sem("count_ready")
        deg_full = sem("deg_full")
        deg_ready = sem("deg_ready")
        rdeg_ready = sem("rdeg_ready")
        mean_ready = sem("mean_ready")
        gin_adj_ready = sem("gin_adj_ready")
        gcn_adj_ready = sem("gcn_adj_ready")
        dve_step = sem("dve_step")
        var_ready = sem("var_ready")
        rstd_ready = sem("rstd_ready")
        normed = sem("normed")
        turned_full = [sem(f"turned_full{h}") for h in range(2)]
        turned_hi = [sem(f"turned_hi{h}") for h in range(2)]
        turned_out = [sem(f"turned_out{h}") for h in range(2)]
        rows_full = [sem(f"rows_full{h}") for h in range(2)]
        rows_out = [sem(f"rows_out{h}") for h in range(2)]
        neigh_full = sem("neigh_full")
        neigh_hi = [sem(f"neigh_hi{h}") for h in range(2)]
        neigh_out = [sem(f"neigh_out{h}") for h in range(2)]
        proj_full = sem("proj_full")
        q_rows = sem("q_rows")
        k_rows = sem("k_rows")
        v_ready = sem("v_ready")
        scores_full = sem("scores_full")
        masked_ready = sem("masked_ready")
        prob_ready = sem("prob_ready")
        probT_full = sem("probT_full")
        probT_ready = sem("probT_ready")
        o_full = sem("o_full")
        o_ready = sem("o_ready")
        up_full = sem("up_full")
        up_rows = sem("up_rows")
        up_act0 = sem("up_act0")
        up_hi = sem("up_hi")
        down_used = sem("down_used")
        up_ready = sem("up_ready")
        diag_ready = sem("diag_ready")
        dinv_full = sem("dinv_full")
        dinv_row_ready = sem("dinv_row_ready")
        res_ready = sem("res_ready")
        max_ready = sem("max_ready")
        lse_ready = sem("lse_ready")

        def hi(name):
            return w_hi[:, G[name] % SPLIT_RING]

        def lo(name):
            return w_lo[:, G[name] % SPLIT_RING]

        def raw_of(name):
            return raw[:, G[name] % RAW_RING]

        def loaded(name, c):
            return w_in[(name, c * PIECES.get(name, 1) // C)], 16

        def lo_made(name, c):
            on_pool = c in LO_ON_POOL[name]
            return (w_lo_pool if on_pool else w_lo_dve), lo_count(name, on_pool, c + 1)

        def two(t):
            return t[:, 0:HALF].rearrange("p (c n) -> p c n", c=2)

        def col(name, c):
            return col_sb[:, COL[name] + c:COL[name] + c + 1]

        def row(name, h=None):
            i = ROW[name]
            return row_sb[:, i, :] if h is None else row_sb[:, i, h * HALF:(h + 1) * HALF]

        def half(t, h):
            return t[:, h * HALF:(h + 1) * HALF]

        def chunk(t, c):
            return t[:, c * P:(c + 1) * P]

        group_used = {"q": (proj_full, 1), "k": (proj_full, 2), "v": (proj_full, 3), "out": (rows_full[1], R_OUT),
                      **{f"up{j}": (up_full, j + 1) for j in range(4)},
                      **{f"down{j}": (down_used, j + 1) for j in range(3)}, "down3": (rows_full[1], R_DOWN),
                      "self": (rows_full[1], R_L1), "neigh": (rows_full[1], R_L1),
                      **{f"gin{i}": (rows_full[1], R_GIN + i) for i in range(GIN)}}

        block = ctx.enter_context(nc.Block())

        @block.sync
        def _(sp):
            sp.dma_start(x_sb[:, :], x).then_inc(x_in, 16)
            for i, name in enumerate(GROUPS):
                if i >= RAW_RING:
                    before = GROUPS[i - RAW_RING]
                    sp.wait_ge(w_lo_pool, lo_count(before, True))
                    sp.wait_ge(w_lo_dve, lo_count(before, False))
                n = PIECES.get(name, 1)
                for p in range(n):
                    cs = slice(p * C // n, (p + 1) * C // n)
                    sp.dma_start(raw[:, i % RAW_RING, cs, :], weights[i, :, cs, :]).then_inc(w_in[(name, p)], 16)
                if name == "v":
                    sp.dma_start(row_sb[:, 0:2, :], rows[0:2, :].partition_broadcast(P)).then_inc(rows_in, 16)
                if name == "up3":
                    sp.dma_start(row_sb[:, 2:, :], rows[2:, :].partition_broadcast(P)).then_inc(late_rows_in, 16)
            for h in range(2):
                sp.wait_ge(normed, 2 * 5 + h + 1)
                sp.dma_start(half(out, h), half(res, h)).then_inc(out_done, 16)
            sp.wait_ge(out_done, 32)

        @block.gpsimd
        def _(pool):
            done = [0]

            def link(ins):
                done[0] += 1
                ins.then_inc(pool_step, 1)
                pool.wait_ge(pool_step, done[0])

            def rsqrt_of_variance(i):
                pool.wait_ge(var_ready, i + 1)
                pool.tensor_tensor(rstd[:, i:i + 1], var[:, i:i + 1], minus_half[:, :], ALU.pow)\
                    .then_inc(rstd_ready, 1)

            def split_lo(name):
                for c in LO_ON_POOL[name]:
                    pool.wait_ge(w_hi_ready, C * G[name] + c + 1)
                    pool.tensor_tensor(lo(name)[:, c, :], raw_of(name)[:, c, :], hi(name)[:, c, :].bitcast(F32),
                                       ALU.subtract).then_inc(w_lo_pool, 1)

            pool.memset(ones[:, :], 1.0).then_inc(ones_ready, 1)
            pool.memset(minus_half[:, :], -0.5)
            link(pool.memset(ident[:, :], 0.0))
            pool.affine_select(out=ident[:, :], in_=ident[:, :], compare_op=ALU.not_equal, fill=1.0, base=0,
                               pattern=[[-1, P]], channel_multiplier=1).then_inc(ident_ready, 1)
            pool.iota(iota[:, :], pattern=[[1, P]], base=0, channel_multiplier=0,
                      allow_small_or_imprecise_dtypes=True).then_inc(iota_ready, 1)
            pool.memset(bias_raw[:, 3 * D:], 0.0).then_inc(bias_zero, 1)
            rsqrt_of_variance(LN1)
            split_lo("q")
            split_lo("k")
            split_lo("v")
            pool.wait_ge(x_in, 16)
            pool.wait_ge(rows_in, 16)
            pool.tensor_tensor(res[:, :], x_sb[:, :], row("b_out"), ALU.add).then_inc(res_ready, 1)
            split_lo("out")
            pool.wait_ge(deg_ready, 1)
            link(pool.tensor_scalar(dinv[:, :], deg[:, P:P + 1], 1.0, None, ALU.add))
            link(pool.tensor_tensor(dinv[:, :], dinv[:, :], minus_half[:, :], ALU.pow))
            pool.wait_ge(ident_ready, 1)
            pool.tensor_scalar(dinv_diag[:, :], ident[:, :], dinv[:, :], None, ALU.mult).then_inc(diag_ready, 1)
            split_lo("up0")
            split_lo("up1")
            split_lo("up2")
            split_lo("up3")
            rsqrt_of_variance(LN2)
            split_lo("down0")
            pool.wait_ge(late_rows_in, 16)
            for h in range(2):
                pool.wait_ge(rows_out[h], R_OUT)
            link(pool.tensor_tensor(res[:, :], x_sb[:, :], row("b_down"), ALU.add))
            pool.tensor_tensor(res[:, :], res[:, :], a_sb[:, :], ALU.add).then_inc(res_ready, 1)
            split_lo("down1")
            pool.wait_ge(eps_in, 16)
            link(pool.tensor_scalar(eps1[:, :], eps1[:, :], 1.0, None, ALU.add))
            link(pool.tensor_tensor(gin_adj[:, :, :], ident[:, :].unsqueeze(1).broadcast_to([P, GIN, P]),
                                    eps1[:, :].unsqueeze(2).broadcast_to([P, GIN, P]), ALU.mult))
            split_lo("down2")
            pool.wait_ge(count_ready, 1)
            pool.tensor_tensor(gin_adj[:, :, :], gin_adj[:, :, :],
                               count[:, :].unsqueeze(1).broadcast_to([P, GIN, P]), ALU.add)\
                .then_inc(gin_adj_ready, 1)
            split_lo("down3")
            pool.wait_ge(rdeg_ready, 1)
            pool.tensor_tensor(mean_adj[:, :], count[:, :], rdeg[:, :], ALU.mult).then_inc(mean_ready, 1)
            split_lo("self")
            split_lo("neigh")
            rsqrt_of_variance(LNX1)
            pool.wait_ge(normed, 2 * 2 + 2)
            pool.tensor_tensor(res[:, :], x1[:, :], row("beta"), ALU.add).then_inc(res_ready, 1)
            split_lo("gin0")
            split_lo("gin1")
            rsqrt_of_variance(LNH)
            rsqrt_of_variance(LNX2)
            split_lo("gin2")
            split_lo("gin3")
            link(pool.tensor_scalar(gcn_adj[:, :], count_i[:, :], dinv[:, :], None, ALU.mult))
            pool.wait_ge(dinv_row_ready, 1)
            pool.tensor_tensor(gcn_adj[:, :], gcn_adj[:, :], dinv_row[:, :], ALU.mult).then_inc(gcn_adj_ready, 1)
            split_lo("gin4")
            split_lo("gcn")
            split_lo("dense")
            rsqrt_of_variance(LNX3)
            pool.wait_ge(normed, 2 * 4 + 2)
            pool.tensor_tensor(res[:, :], xn[:, :], row("b_dense"), ALU.add).then_inc(res_ready, 1)
            rsqrt_of_variance(LNX4)

        @block.scalar
        def _(act):
            act.dma_start(edge_i[:, :], edges).then_inc(edges_in, 16)
            act.dma_start(col_sb[:, :], cols).then_inc(cols_in, 16)
            act.dma_start(eps1[:, :], eps.partition_broadcast(P)).then_inc(eps_in, 16)
            act.preload_act_table_set("natural_log_exp_and_others")

            def split_hi(name, cs):
                i = G[name]
                if cs[0] == 0 and i >= SPLIT_RING:
                    act.wait_ge(*group_used[GROUPS[i - SPLIT_RING]])
                act.wait_ge(*loaded(name, cs[-1]))
                lo_c, hi_c = cs[0], cs[-1] + 1
                act.activation(hi(name)[:, lo_c:hi_c, :], raw_of(name)[:, lo_c:hi_c, :], ACT.Copy)\
                    .then_inc(w_hi_ready, len(cs))

            def split_hi_group(name):
                split_hi(name, [0, 1])
                split_hi(name, [2, 3])

            def turned_hi_parts(n, scale=None, bias=None, halves=range(2)):
                for h in halves:
                    act.wait_ge(turned_full[h], n)
                    if bias is None:
                        ins = act.activation(xT_hi[:, 2 * h:2 * h + 2, :], two(T[h]), ACT.Copy)
                    else:
                        for c in range(2):
                            ins = act.activation(xT_hi[:, 2 * h + c, :], chunk(T[h], c), ACT.Identity,
                                                 bias=bias(2 * h + c), scale=1.0 if scale is None else scale(2 * h + c))
                    ins.then_inc(turned_hi[h], 1)

            def heads_turned(n, dst, bias):
                act.wait_ge(turned_full[0], n)
                for c in range(2):
                    ins = act.activation(dst[:, c, :], chunk(T[0], c), ACT.Identity, bias=bias(c))
                ins.then_inc(turned_out[0], 1)

            split_hi("q", [0])
            split_hi("q", [1])
            act.wait_ge(cols_in, 16)
            turned_hi_parts(T_LN1, lambda c: col("ln1_w", c), lambda c: col("ln1_b", c), halves=[0])
            split_hi("q", [2])
            split_hi("q", [3])
            split_hi_group("k")
            act.wait_ge(proj_full, 1)
            act.activation(q_sb[:, :], U[0][:, :], ACT.Copy).then_inc(q_rows, 1)
            split_hi_group("v")
            act.wait_ge(proj_full, 2)
            act.activation(k_sb[:, :], U[1][:, :], ACT.Copy).then_inc(k_rows, 1)
            act.wait_ge(bias_zero, 2)
            act.dma_start(bias_raw[0:33:32, :], bias_rows.partition_broadcast(2)).then_inc(bias_in, 16)
            heads_turned(T_Q, qT, lambda c: col("b_q", c))
            split_hi_group("out")
            heads_turned(T_K, kT, lambda c: col("b_k", c))
            split_hi_group("up0")
            for i, h in enumerate(HEAD_ORDER):
                act.wait_ge(masked_ready, i + 1)
                act.activation(prob[:, h, :], masked[:, h, :], ACT.Exp, bias=neg_max[:, h:h + 1], scale=-1.0,
                               accum_out=sums[:, h:h + 1]).then_inc(prob_ready, 1)
            split_hi_group("up1")
            act.wait_ge(bias_in, 16)
            act.activation(bias_hl[:, :], bias_raw[:, :], ACT.Copy).then_inc(bias_hi_ready, 1)
            turned_hi_parts(T_O)
            split_hi_group("up2")
            split_hi_group("up3")
            turned_hi_parts(T_LN2, lambda c: col("ln2_w", c), lambda c: col("ln2_b", c), halves=[0])
            split_hi_group("down0")

            def up_to_sbuf(j):
                act.wait_ge(up_full, j + 1)
                if j >= 2:
                    act.wait_ge(turned_full[1], T_UP + j - 2)
                act.activation(up[:, j % 2, :], U[j][:, :], ACT.Copy).then_inc(up_rows, 1)

            def up_turned(j):
                act.wait_ge(turned_full[0], T_UP + j)
                if j >= 2:
                    act.wait_ge(up_ready, j - 1)
                for c in range(2):
                    ins = act.activation(up_act[:, j % 2, c, :], chunk(T[0], c), ACT.Relu, bias=col("b_up", C * j + c))
                ins.then_inc(turned_out[0], 1)

            up_to_sbuf(0)
            split_hi_group("down1")
            up_to_sbuf(1)
            up_turned(0)
            split_hi_group("down2")
            up_to_sbuf(2)
            up_turned(1)
            split_hi_group("down3")
            up_to_sbuf(3)
            up_turned(2)
            split_hi_group("self")
            up_turned(3)
            split_hi_group("neigh")
            split_hi_group("gin0")
            split_hi_group("gin1")
            turned_hi_parts(T_X1)
            for h in range(2):
                act.wait_ge(neigh_full, h + 1)
                act.activation(nT_hi[:, 2 * h:2 * h + 2, :], two(U[h]), ACT.Copy).then_inc(neigh_hi[h], 1)
            split_hi_group("gin2")
            for i in range(GIN):
                turned_hi_parts(T_GIN + i)
                if i < 4:
                    split_hi_group(["gin3", "gin4", "gcn", "dense"][i])
                act.wait_ge(rows_full[0], R_GIN + i)
                act.activation(half(h_sb, 0), R[0][:, 0:HALF], ACT.Relu).then_inc(rows_out[0], 1)
            act.wait_ge(max_ready, 1)
            act.activation(a_sb[:, :], h_sb[:, :], ACT.Exp, bias=lsm[:, 1:2], accum_out=lsm[:, 2:3])\
                .then_inc(lse_ready, 1)
            act.wait_ge(lse_ready, 1)
            act.activation(lsm[:, 3:4], lsm[:, 2:3], ACT.Ln).then_inc(lse_ready, 1)
            turned_hi_parts(T_X3)
            act.wait_ge(rows_full[0], R_GCN)
            act.activation(half(h_sb, 0), R[0][:, 0:HALF], ACT.Copy).then_inc(rows_out[0], 1)
            turned_hi_parts(T_AGG, None, lambda c: col("b_gcn", c), halves=[0])

        @block.tensor
        def _(pe):
            def turn(n, src, ready, first):
                for h in range(2):
                    pe.wait_ge(ready, first + h)
                    if n > 1:
                        pe.wait_ge(turned_out[h], n - 1)
                    for c in range(2):
                        ins = pe.transpose(chunk(T[h], c), chunk(src, 2 * h + c), ident[:, :])
                    ins.then_inc(turned_full[h], 1)

            def aggregate(n, src, adj, ready, first, then=None):
                for h in range(2):
                    pe.wait_ge(ready[h], first[h])
                    pe.wait_ge(turned_out[h], n - 1)
                    for c in range(2):
                        ins = pe.matmul(chunk(T[h], c), chunk(src, 2 * h + c), adj, start=True, stop=True)
                    ins.then_inc(turned_full[h], 1)
                    if then is not None:
                        then(h)

            def weights_there(name, c):
                pe.wait_ge(w_hi_ready, C * G[name] + c + 1)
                pe.wait_ge(*lo_made(name, c))

            def product(out, name, cols, x_hi, x_lo, start=True, stop=True, hi_there=None, lo_there=None):
                for c in range(C):
                    if hi_there is not None:
                        hi_there(c)
                        weights_there(name, c)
                    pe.matmul(out, x_hi[:, c, :], hi(name)[:, c, cols], start=(start and c == 0), stop=False)
                    pe.matmul(out, x_hi[:, c, :], lo(name)[:, c, cols], start=False, stop=False)
                for c in range(C):
                    if lo_there is not None:
                        lo_there(c)
                    ins = pe.matmul(out, x_lo[:, c, :], hi(name)[:, c, cols], start=False, stop=(stop and c == C - 1))
                return ins

            def turned_there(n):
                def hi_there(c):
                    if c % 2 == 0:
                        pe.wait_ge(turned_hi[c // 2], HI_FILLS.index(n) + 1)

                def lo_there(c):
                    if c % 2 == 0:
                        pe.wait_ge(turned_out[c // 2], n)
                return hi_there, lo_there

            def bias_row(name, r, h):
                i = BIAS.index(name) * D
                pe.wait_ge(rows_out[h], r - 1)
                pe.matmul(R[h][:, 0:HALF], ones_r[:, :], bias_hl[:, i + h * HALF:i + (h + 1) * HALF],
                          start=True, stop=False)

            def row_halves(r, n, name, x_hi, x_lo, there=None, last=True, follows=False):
                hi_there, lo_there = there or turned_there(n)
                for h in range(2):
                    if not follows and r > 1:
                        pe.wait_ge(rows_out[h], r - 1)
                    ins = product(R[h][:, 0:HALF], name, slice(h * HALF, (h + 1) * HALF), x_hi, x_lo,
                                  start=not follows, stop=last,
                                  hi_there=hi_there if h == 0 else None, lo_there=lo_there if h == 0 else None)
                    if last:
                        ins.then_inc(rows_full[h], 1)

            def project(i, name, cs):
                hi_there, lo_there = turned_there(T_LN1)
                for c in cs:
                    if i == 0:
                        hi_there(c)
                    pe.wait_ge(w_hi_ready, C * G[name] + c + 1)
                    pe.matmul(U[i][:, :], xT_hi[:, c, :], hi(name)[:, c, :], start=(c == 0), stop=False)
                for c in (sorted(cs, key=lambda c: c < 2) if i == 0 else cs):
                    if i == 0:
                        lo_there(c)
                    pe.matmul(U[i][:, :], xT_lo[:, c, :], hi(name)[:, c, :], start=False, stop=False)
                for c in cs:
                    pe.wait_ge(*lo_made(name, c))
                    ins = pe.matmul(U[i][:, :], xT_hi[:, c, :], lo(name)[:, c, :], start=False, stop=(c == C - 1))
                if cs[-1] == C - 1:
                    ins.then_inc(proj_full, 1)

            def keep_warm(n):
                for _ in range(n):
                    pe.matmul(T[0][:, HALF:HALF + P], ones[:, :], ones[:, :], start=True, stop=True)

            def turn_rows(n, src, ready):
                pe.wait_ge(ready, 1)
                for h in range(2):
                    pe.wait_ge(turned_out[h], n - 1)
                    for c in range(2):
                        ins = pe.transpose(chunk(T[h], c), chunk(src, 2 * h + c), ident[:, :])
                    ins.then_inc(turned_full[h], 1)

            pe.wait_ge(ones_ready, 1)
            keep_warm(WARM["start"])
            pe.wait_ge(ident_ready, 1)
            turn(T_LN1, xn, normed, 1)
            project(0, "q", range(C))
            project(1, "k", range(C))
            turn_rows(T_Q, q_sb, q_rows)
            project(2, "v", range(0, 2))
            turn_rows(T_K, k_sb, k_rows)
            project(2, "v", range(2, C))
            pe.wait_ge(src_ready, 1)
            pe.wait_ge(dst_ready, 1)
            for e in range(EC):
                ins = pe.matmul(U[3][:, 0:P], hot_src[:, e, :], hot_dst[:, e, :], start=(e == 0), stop=(e == EC - 1))
            ins.then_inc(count_full, 1)

            score_bank = [R[0], R[1], U[0], U[1]]
            for h in range(HEADS):
                if h % 4 == 0:
                    pe.wait_ge(turned_out[h // 4], T_K)
                at_row = (h % 2) * DH
                b = score_bank[2 * (h // 4) + h % 2]
                at = (h % 4) // 2
                ins = pe.matmul(b[:, at * P:(at + 1) * P], qT[at_row:at_row + DH, h // 2, :],
                                kT[at_row:at_row + DH, h // 2, :], start=True, stop=True)
                if h % 4 >= 2:
                    ins.then_inc(scores_full, 1)
            pe.wait_ge(count_ready, 1)
            pe.wait_ge(ones_ready, 1)
            pe.matmul(U[3][:, 0:P], ones[:, :], count[:, :], start=True, stop=True)
            pe.matmul(U[3][:, P:P + 1], count[:, :], ones[:, 0:1], start=True, stop=True).then_inc(deg_full, 1)

            prob_bank = [U[3], U[2], R[0], R[1]]

            def turn_prob(i):
                if i == 0:
                    pe.wait_ge(deg_ready, 1)
                if i == 1:
                    pe.wait_ge(v_ready, 1)
                pe.wait_ge(prob_ready, 2 * i + 2)
                for k in range(2):
                    ins = pe.transpose(chunk(prob_bank[i], k), prob[:, HEAD_ORDER[2 * i + k], :], ident[:, :])
                ins.then_inc(probT_full, 1)

            def attend(i):
                pe.wait_ge(probT_ready, i + 1)
                for h in HEAD_ORDER[2 * i:2 * i + 2]:
                    ins = pe.matmul(U[h // 4][:, (h % 4) * DH:(h % 4 + 1) * DH], probT[:, h, :],
                                    v_sb[:, h * DH:(h + 1) * DH], start=True, stop=True)
                if i % 2:
                    ins.then_inc(o_full, 1)

            turn_prob(0)
            turn_prob(1)
            turn_prob(2)
            attend(0)
            attend(1)
            turn_prob(3)
            attend(2)
            attend(3)
            turn(T_O, o_sb, o_ready, 1)
            row_halves(R_OUT, T_O, "out", xT_hi, xT_lo)
            keep_warm(WARM["ln2"])
            pe.wait_ge(diag_ready, 1)
            pe.matmul(U[3][:, 0:P], ones[:, :], dinv_diag[:, :], start=True, stop=True).then_inc(dinv_full, 1)
            turn(T_LN2, xn, normed, 3)

            def up_block(j):
                hi_there, lo_there = turned_there(T_LN2)
                if j == 3:
                    pe.wait_ge(dinv_row_ready, 1)
                product(U[j][:, :], f"up{j}", slice(0, D), xT_hi, xT_lo, hi_there=hi_there, lo_there=lo_there)\
                    .then_inc(up_full, 1)

            def turn_up(j):
                pe.wait_ge(up_rows, j + 1)
                for h in range(2):
                    pe.wait_ge(turned_out[h], T_UP + j - 1)
                    for c in range(2):
                        ins = pe.transpose(chunk(T[h], c), up[:, j % 2, (2 * h + c) * P:(2 * h + c + 1) * P], ident[:, :])
                    ins.then_inc(turned_full[h], 1)

            def down_block(j):
                def hi_there(c):
                    if c == 0:
                        pe.wait_ge(up_hi, j + 1)

                def lo_there(c):
                    if c == 0:
                        pe.wait_ge(up_ready, j + 1)
                for h in range(2):
                    if j == 0:
                        pe.wait_ge(rows_out[h], R_DOWN - 1)
                    ins = product(R[h][:, 0:HALF], f"down{j}", slice(h * HALF, (h + 1) * HALF),
                                  upT_hi[:, C * j:C * j + C, :], upT_lo[:, C * j:C * j + C, :],
                                  start=(j == 0), stop=(j == 3), hi_there=hi_there if h == 0 else None,
                                  lo_there=lo_there if h == 0 else None)
                    if j == 3:
                        ins.then_inc(rows_full[h], 1)
                if j < 3:
                    ins.then_inc(down_used, 1)

            up_block(0)
            up_block(1)
            turn_up(0)
            up_block(2)
            turn_up(1)
            up_block(3)
            turn_up(2)
            down_block(0)
            turn_up(3)
            down_block(1)
            down_block(2)
            down_block(3)

            keep_warm(WARM["x1"])
            pe.wait_ge(bias_ready, 1)
            pe.wait_ge(ones_r_ready, 1)
            for h in range(2):
                bias_row("l1", R_L1, h)
            turn(T_X1, x1, normed, 5)
            pe.wait_ge(mean_ready, 1)
            for h in range(2):
                for c in range(2):
                    ins = pe.matmul(chunk(U[h], c), chunk(x1, 2 * h + c), mean_adj[:, :], start=True, stop=True)
                ins.then_inc(neigh_full, 1)
            row_halves(R_L1, T_X1, "self", xT_hi, xT_lo, last=False, follows=True)

            def neigh_hi_there(c):
                if c % 2 == 0:
                    pe.wait_ge(neigh_hi[c // 2], 1)

            def neigh_lo_there(c):
                if c % 2 == 0:
                    pe.wait_ge(neigh_out[c // 2], 1)
            row_halves(R_L1, None, "neigh", nT_hi, nT_lo, there=(neigh_hi_there, neigh_lo_there), follows=True)

            keep_warm(WARM["x2"])
            pe.wait_ge(gin_adj_ready, 1)
            for i in range(GIN):
                src, ready, first = (xn, [normed, normed], [7, 8]) if i == 0 else (h_sb, rows_out, [R_GIN + i - 1] * 2)
                aggregate(T_GIN + i, src, gin_adj[:, i, :], ready, first,
                          then=lambda h: bias_row(f"gin{i}", R_GIN + i, h))
                row_halves(R_GIN + i, T_GIN + i, f"gin{i}", xT_hi, xT_lo, follows=True)

            keep_warm(WARM["x3"])
            turn(T_X3, xn, normed, 9)
            row_halves(R_GCN, T_X3, "gcn", xT_hi, xT_lo)
            pe.wait_ge(gcn_adj_ready, 1)
            aggregate(T_AGG, h_sb, gcn_adj[:, :], rows_out, [R_GCN] * 2)
            row_halves(R_DENSE, T_AGG, "dense", xT_hi, xT_lo)

        @block.vector
        def _(dve):
            done = [0]

            def mark(ins):
                done[0] += 1
                ins.then_inc(dve_step, 1)

            def link(ins):
                mark(ins)
                dve.wait_ge(dve_step, done[0])

            def stats(i, h, src):
                mark(dve.bn_stats(stat[:, i, h, :], src))

            def mean_and_variance(i):
                dve.wait_ge(dve_step, done[0])
                link(dve.bn_aggr(mv[:, i, :], stat[:, i, :, :].rearrange("p a b -> p (a b)")))
                dve.tensor_scalar(var[:, i:i + 1], mv[:, i, 1:2], LN_EPS, None, ALU.add).then_inc(var_ready, 1)

            def mean_and_rstd(i):
                mean_and_variance(i)
                dve.wait_ge(rstd_ready, i + 1)

            def apply(i, src, dst):
                for h in range(2):
                    dve.tensor_scalar(half(dst, h), half(src, h), mv[:, i, 0:1], rstd[:, i:i + 1],
                                      ALU.subtract, ALU.mult).then_inc(normed, 1)

            def split_lo(name):
                for c in range(C):
                    if c not in LO_ON_POOL[name]:
                        dve.wait_ge(w_hi_ready, C * G[name] + c + 1)
                        dve.tensor_tensor(lo(name)[:, c, :], raw_of(name)[:, c, :], hi(name)[:, c, :].bitcast(F32),
                                          ALU.subtract).then_inc(w_lo_dve, 1)

            def turned_lo_parts(n):
                for h in range(2):
                    dve.wait_ge(turned_full[h], n)
                    dve.wait_ge(turned_hi[h], HI_FILLS.index(n) + 1)
                    dve.tensor_tensor(xT_lo[:, 2 * h:2 * h + 2, :], two(T[h]),
                                      xT_hi[:, 2 * h:2 * h + 2, :].bitcast(F32), ALU.subtract)\
                        .then_inc(turned_out[h], 1)

            def turned_affine_parts(n, scale, bias):
                for h in (1, 0):
                    pair = slice(2 * h, 2 * h + 2)
                    dve.wait_ge(turned_full[h], n)
                    if h == 0:
                        dve.wait_ge(turned_hi[0], HI_FILLS.index(n) + 1)
                    for c in range(2 * h, 2 * h + 2):
                        if scale is None:
                            mark(dve.tensor_scalar(xT[:, c, :], chunk(T[h], c % 2), bias(c), None, ALU.add))
                        else:
                            mark(dve.tensor_scalar(xT[:, c, :], chunk(T[h], c % 2), scale(c), bias(c),
                                                   ALU.mult, ALU.add))
                    dve.wait_ge(dve_step, done[0])
                    if h == 1:
                        dve.tensor_copy(xT_hi[:, pair, :], xT[:, pair, :]).then_inc(turned_hi[1], 1)
                        dve.wait_ge(turned_hi[1], HI_FILLS.index(n) + 1)
                    dve.tensor_tensor(xT_lo[:, pair, :], xT[:, pair, :], xT_hi[:, pair, :].bitcast(F32),
                                      ALU.subtract).then_inc(turned_out[h], 1)

            def heads_turned(n, dst, bias):
                dve.wait_ge(turned_full[1], n)
                for c in range(2, 4):
                    ins = dve.tensor_scalar(dst[:, c, :], chunk(T[1], c - 2), bias(c), None, ALU.add)
                ins.then_inc(turned_out[1], 1)

            dve.memset(ones_r[:, :].bitcast(F32), 1.0).then_inc(ones_r_ready, 1)
            dve.memset(bias_raw[:, 0:3 * D], 0.0).then_inc(bias_zero, 1)
            dve.wait_ge(x_in, 16)
            for h in range(2):
                stats(LN1, h, half(x_sb, h))
            mean_and_rstd(LN1)
            apply(LN1, x_sb, xn)
            dve.wait_ge(edges_in, 16)
            link(dve.tensor_copy(edge_f[:, :], edge_i[:, :]))
            dve.wait_ge(cols_in, 16)
            turned_affine_parts(T_LN1, lambda c: col("ln1_w", c), lambda c: col("ln1_b", c))
            split_lo("q")
            dve.wait_ge(iota_ready, 1)

            def one_hot(dst, at):
                return dve.tensor_tensor(dst[:, :, :], iota[:, :].unsqueeze(1).broadcast_to([P, EC, P]),
                                         edge_f[:, at:at + EC].unsqueeze(2).broadcast_to([P, EC, P]), ALU.is_equal)
            one_hot(hot_src, 0).then_inc(src_ready, 1)
            split_lo("k")
            split_lo("v")
            one_hot(hot_dst, EC).then_inc(dst_ready, 1)
            heads_turned(T_Q, qT, lambda c: col("b_q", c))
            heads_turned(T_K, kT, lambda c: col("b_k", c))
            split_lo("out")
            dve.wait_ge(proj_full, 3)
            dve.wait_ge(rows_in, 16)
            dve.tensor_tensor(v_sb[:, :], U[2][:, :], row("b_v"), ALU.add).then_inc(v_ready, 1)
            dve.wait_ge(count_full, 1)
            dve.wait_ge(ident_ready, 1)
            mark(dve.tensor_tensor(count_i[:, :], U[3][:, 0:P], ident[:, :], ALU.add))
            dve.tensor_copy(count[:, :], U[3][:, 0:P]).then_inc(count_ready, 1)
            dve.wait_ge(dve_step, done[0])
            link(dve.tensor_scalar(mask[:, :], count_i[:, :], 0.0, -NEG * DH ** 0.5, ALU.is_equal, ALU.mult))
            score_bank = [R[0], R[1], U[0], U[1]]
            for i, h in enumerate(HEAD_ORDER):
                if i % 2 == 0:
                    dve.wait_ge(scores_full, i // 2 + 1)
                if i == 2:
                    dve.wait_ge(deg_full, 1)
                    dve.tensor_copy(deg[:, :], U[3][:, 0:P + 1]).then_inc(deg_ready, 1)
                dve.tensor_tensor_reduce(masked[:, h, :], chunk(score_bank[i // 2], i % 2), mask[:, :],
                                         -(DH ** -0.5), 3.0e38, ALU.add, ALU.min,
                                         neg_max[:, h:h + 1]).then_inc(masked_ready, 1)
            prob_bank = [U[3], U[2], R[0], R[1]]

            def probT_to_sbuf(i):
                dve.wait_ge(probT_full, i + 1)
                h = HEAD_ORDER[2 * i]
                dve.tensor_copy(probT[:, h:h + 3:2, :], two(prob_bank[i])).then_inc(probT_ready, 1)

            def normalise_o(g):
                dve.wait_ge(prob_ready, 4 * g + 4)
                link(dve.reciprocal(rsum[:, 4 * g:4 * g + 4], sums[:, 4 * g:4 * g + 4]))
                dve.wait_ge(o_full, g + 1)
                dve.tensor_tensor(half(o_sb, g).rearrange("p (h d) -> p h d", h=4),
                                  U[g][:, 0:HALF].rearrange("p (h d) -> p h d", h=4),
                                  rsum[:, 4 * g:4 * g + 4].unsqueeze(2).broadcast_to([P, 4, DH]),
                                  ALU.mult).then_inc(o_ready, 1)

            probT_to_sbuf(0)
            probT_to_sbuf(1)
            probT_to_sbuf(2)
            normalise_o(0)
            probT_to_sbuf(3)
            normalise_o(1)
            turned_lo_parts(T_O)
            split_lo("up0")
            split_lo("up1")
            dve.wait_ge(res_ready, 1)
            for h in range(2):
                dve.wait_ge(rows_full[h], R_OUT)
                dve.tensor_tensor(half(a_sb, h), R[h][:, 0:HALF], half(res, h), ALU.add).then_inc(rows_out[h], 1)
                dve.wait_ge(rows_out[h], R_OUT)
                stats(LN2, h, half(a_sb, h))
            mean_and_rstd(LN2)
            apply(LN2, a_sb, xn)
            dve.wait_ge(dinv_full, 1)
            dve.tensor_copy(dinv_row[:, :], U[3][:, 0:P]).then_inc(dinv_row_ready, 1)
            turned_affine_parts(T_LN2, lambda c: col("ln2_w", c), lambda c: col("ln2_b", c))
            split_lo("up2")
            split_lo("up3")
            link(dve.tensor_scalar(rdeg[:, :], deg[:, 0:P], 1.0, None, ALU.max))
            dve.reciprocal(rdeg[:, :], rdeg[:, :]).then_inc(rdeg_ready, 1)
            split_lo("down0")

            def up_turned(j):
                dve.wait_ge(turned_full[1], T_UP + j)
                for c in range(2, C):
                    ins = dve.tensor_scalar(up_act[:, j % 2, c, :], chunk(T[1], c - 2), col("b_up", C * j + c), 0.0,
                                            ALU.add, ALU.max)
                ins.then_inc(turned_out[1], 1)
                for h in range(2):
                    dve.wait_ge(turned_out[h], T_UP + j)
                block_hi, block_lo = upT_hi[:, C * j:C * j + C, :], upT_lo[:, C * j:C * j + C, :]
                dve.tensor_copy(block_hi, up_act[:, j % 2, :, :]).then_inc(up_hi, 1)
                dve.wait_ge(up_hi, j + 1)
                dve.tensor_tensor(block_lo, up_act[:, j % 2, :, :], block_hi.bitcast(F32), ALU.subtract)\
                    .then_inc(up_ready, 1)

            up_turned(0)
            split_lo("down1")
            dve.wait_ge(bias_hi_ready, 1)
            dve.tensor_tensor(bias_hl[32:33, :], bias_raw[32:33, :], bias_hl[32:33, :].bitcast(F32), ALU.subtract)\
                .then_inc(bias_ready, 1)
            up_turned(1)
            split_lo("down2")
            up_turned(2)
            split_lo("down3")
            up_turned(3)
            split_lo("self")
            split_lo("neigh")
            dve.wait_ge(res_ready, 2)
            for h in range(2):
                dve.wait_ge(rows_full[h], R_DOWN)
                dve.tensor_tensor(half(x1, h), R[h][:, 0:HALF], half(res, h), ALU.add).then_inc(rows_out[h], 1)
                dve.wait_ge(rows_out[h], R_DOWN)
                stats(LNX1, h, half(x1, h))
            mean_and_rstd(LNX1)
            apply(LNX1, x1, x1)
            turned_lo_parts(T_X1)
            for h in range(2):
                dve.wait_ge(neigh_hi[h], 1)
                dve.tensor_tensor(nT_lo[:, 2 * h:2 * h + 2, :], two(U[h]), nT_hi[:, 2 * h:2 * h + 2, :].bitcast(F32),
                                  ALU.subtract).then_inc(neigh_out[h], 1)
            split_lo("gin0")
            for h in range(2):
                dve.wait_ge(rows_full[h], R_L1)
                stats(LNH, h, R[h][:, 0:HALF])
            mean_and_variance(LNH)
            dve.wait_ge(res_ready, 3)
            for h in range(2):
                dve.scalar_tensor_tensor(half(xn, h), R[h][:, 0:HALF], mv[:, LNH, 0:1], row("gamma", h),
                                         ALU.subtract, ALU.mult).then_inc(rows_out[h], 1)
            dve.wait_ge(rstd_ready, LNH + 1)
            for h in range(2):
                dve.wait_ge(rows_out[h], R_L1)
                link(dve.scalar_tensor_tensor(half(xn, h), half(xn, h), rstd[:, LNH:LNH + 1], half(res, h),
                                              ALU.mult, ALU.add))
                stats(LNX2, h, half(xn, h))
            mean_and_rstd(LNX2)
            apply(LNX2, xn, xn)
            for i in range(GIN):
                turned_lo_parts(T_GIN + i)
                for name in [["gin1", "gin2"], ["gin3"], ["gin4"], ["gcn"], ["dense"]][i]:
                    split_lo(name)
                dve.wait_ge(rows_full[1], R_GIN + i)
                dve.tensor_scalar(half(h_sb, 1), R[1][:, 0:HALF], 0.0, None, ALU.max).then_inc(rows_out[1], 1)
            for h in range(2):
                dve.wait_ge(rows_out[h], R_GIN + GIN - 1)
            link(dve.tensor_reduce(lsm[:, 0:1], h_sb[:, :], AX_X, ALU.max))
            dve.tensor_scalar(lsm[:, 1:2], lsm[:, 0:1], -1.0, None, ALU.mult).then_inc(max_ready, 1)
            for h in range(2):
                link(dve.tensor_tensor(half(xn, h), half(h_sb, h), half(xn, h), ALU.add))
                stats(LNX3, h, half(xn, h))
            mean_and_variance(LNX3)
            dve.wait_ge(lse_ready, 2)
            link(dve.tensor_tensor(lsm[:, 4:5], lsm[:, 0:1], lsm[:, 3:4], ALU.add))
            mark(dve.tensor_tensor(mv[:, LNX3, 0:1], mv[:, LNX3, 0:1], lsm[:, 4:5], ALU.subtract))
            for h in range(2):
                mark(dve.tensor_scalar(half(xn, h), half(xn, h), lsm[:, 4:5], None, ALU.subtract))
            dve.wait_ge(dve_step, done[0])
            dve.wait_ge(rstd_ready, LNX3 + 1)
            apply(LNX3, xn, xn)
            turned_lo_parts(T_X3)
            dve.wait_ge(rows_full[1], R_GCN)
            dve.tensor_copy(half(h_sb, 1), R[1][:, 0:HALF]).then_inc(rows_out[1], 1)
            turned_affine_parts(T_AGG, None, lambda c: col("b_gcn", c))
            dve.wait_ge(res_ready, 4)
            for h in range(2):
                dve.wait_ge(rows_full[h], R_DENSE)
                link(dve.tensor_tensor(half(res, h), R[h][:, 0:HALF], half(res, h), ALU.add))
                stats(LNX4, h, half(res, h))
            mean_and_rstd(LNX4)
            apply(LNX4, res, res)


def kernel(**inputs):
    import numpy as np
    import concourse.bacc as bacc
    from concourse.bass_utils import run_bass_kernel_spmd as run

    a = {k: np.asarray(v) for k, v in inputs.items()}
    w_in, w1, w2 = a["L0_gnn_w_in"], a["L0_gnn_w1"], a["L0_gnn_w2"]
    by_name = {"q": w_in[0:D].T, "k": w_in[D:2 * D].T, "v": w_in[2 * D:3 * D].T, "out": a["L0_gnn_w_out"].T,
               "self": a["L1_gnn_W_self"].T, "neigh": a["L1_gnn_W_neigh"].T, "gin0": a["L2_gnn_W1"],
               "gcn": a["L3_gnn_W_gcn"], "dense": a["L3_gnn_W_dense"]}
    for j in range(4):
        by_name[f"up{j}"] = w1[j * D:(j + 1) * D].T
        by_name[f"down{j}"] = w2.T[j * D:(j + 1) * D]
        by_name[f"gin{j + 1}"] = a["L2_gnn_Ws"][j]
    weights = np.stack([by_name[g].reshape(C, P, D).transpose(1, 0, 2) for g in GROUPS])
    b_in = a["L0_gnn_b_in"]
    columns = {"ln1_w": a["L0_gnn_ln1_w"], "ln1_b": a["L0_gnn_ln1_b"], "b_q": b_in[0:D], "b_k": b_in[D:2 * D],
               "ln2_w": a["L0_gnn_ln2_w"], "ln2_b": a["L0_gnn_ln2_b"], "b_up": a["L0_gnn_b1"],
               "b_gcn": a["L3_gnn_b_gcn"]}
    cols = np.concatenate([columns[name].reshape(-1, P).T for name, _ in COLS], axis=1)
    all_rows = {"b_v": b_in[2 * D:3 * D], "b_out": a["L0_gnn_b_out"], "b_down": a["L0_gnn_b2"],
                "gamma": a["L1_gnn_gamma"], "beta": a["L1_gnn_beta"], "b_dense": a["L3_gnn_b_dense"]}
    rows = np.stack([all_rows[name] for name in ROWS])
    bias_rows = np.concatenate([a["L1_gnn_bias"], a["L2_gnn_b1"], a["L2_gnn_bs"].reshape(-1)]).reshape(1, -1)
    edges = np.concatenate([a["src"].reshape(P, EC), a["dst"].reshape(P, EC)], axis=1)
    arrays = {"x": a["x"], "edges": edges, "cols": cols, "rows": rows, "bias_rows": bias_rows,
              "eps": a["L2_gnn_eps"], "weights": weights}
    arrays = {f"in_{k}": np.ascontiguousarray(v) for k, v in arrays.items()}

    nc = bacc.Bacc("TRN2", target_bir_lowering=False, num_devices=1)
    args = [nc.dram_tensor(k, v.shape, mybir.dt.from_np(v.dtype), kind="ExternalInput").ap()
            for k, v in arrays.items()]
    result = nc.dram_tensor("out_x", (P, D), F32, kind="ExternalOutput").ap()
    residual_gnn(nc, *args, result)
    got = run(nc, [arrays], core_ids=[0])
    return got.results[0]["out_x"]
```

```python
from contextlib import ExitStack

import concourse.bass as bass
from concourse import mybir

ALU = mybir.AluOpType
ACT = mybir.ActivationFunctionType
F32 = mybir.dt.float32
F32R = mybir.dt.float32r
BF16 = mybir.dt.bfloat16
I32 = mybir.dt.int32

P = 128
D = 512
C = D // P
HALF = D // 2
HEADS = 8
DH = D // HEADS
FF = 4 * D
EDGES = 2 * 1024 + P
EC = EDGES // P
GIN = 5
LN_EPS = 1e-5
NEG = 1e9
WARM = {"start": 10, "ln2": 7, "x1": 8, "x2": 18, "x3": 11}
RAW_RING = 5
SPLIT_RING = 5

GROUPS = (["q", "k", "v", "out"] + [f"up{j}" for j in range(4)] + [f"down{j}" for j in range(4)]
          + ["self", "neigh"] + [f"gin{i}" for i in range(GIN)] + ["gcn", "dense"])
G = {name: i for i, name in enumerate(GROUPS)}
PIECES = {"q": 4, "k": 2, "v": 2, "out": 2}

COLS = [("ln1_w", C), ("ln1_b", C), ("b_q", C), ("b_k", C), ("b_up", FF // P)]
COL = {}
for _name, _n in COLS:
    COL[_name] = sum(n for m, n in COLS[:[m for m, _ in COLS].index(_name)])
NCOL = sum(n for _, n in COLS)
ROWS = ["gamma", "beta", "b_dense"]
ROW = {name: i for i, name in enumerate(ROWS)}
BK = 64
LO_AT = BK // 2
BIAS = ["v", "ln2_w", "ln2_b", "out", "down", "l1"] + [f"gin{i}" for i in range(GIN)] + ["gcn", "dense"]
NB = len(BIAS)

LO_ON_POOL = {name: (0, 1) for name in GROUPS}
LO_ON_POOL["v"] = (0, 1, 2)
LO_ON_POOL["out"] = (0, 1, 2)
LO_ON_POOL["up0"] = (0, 1, 2)


def lo_count(name, on_pool, upto=C):
    return sum((k in LO_ON_POOL[g]) == on_pool for g in GROUPS[:G[name] + 1]
               for k in range(upto if g == name else C))


DST_ON_POOL = 3

HEAD_ORDER = [0, 2, 1, 3, 4, 6, 5, 7]

LN1, LN2, LNX1, LNH, LNX2, LNX3, LNX4 = range(7)
(T_LN1, T_Q, T_K, T_O, T_LN2, T_UP, T_X1, T_GIN, T_X3, T_AGG) = (1, 2, 3, 4, 5, 6, 10, 11, 16, 17)
HI_FILLS = [T_LN1, T_O, T_LN2, T_X1, *range(T_GIN, T_GIN + GIN), T_X3, T_AGG]
(R_OUT, R_DOWN, R_L1, R_GIN, R_GCN, R_DENSE) = (1, 2, 3, 4, 9, 10)


def residual_gnn(nc, x, edges, cols, rows, bias_rows, eps, weights, out):
    with ExitStack() as ctx:
        def sb(name, shape, dt=F32):
            return ctx.enter_context(nc.sbuf_tensor(name, shape, dt))

        def sem(name):
            return ctx.enter_context(nc.semaphore(name))

        bank = [ctx.enter_context(nc.psum_tensor(f"bank{i}", [P, 512], F32)) for i in range(8)]
        T, R, U = bank[0:2], bank[2:4], bank[4:8]
        K_TURNED = [R[0], U[0]]

        raw = sb("raw", [P, RAW_RING, C, D])
        w_hi = sb("w_hi", [P, SPLIT_RING, C, D], F32R)
        w_lo = sb("w_lo", [P, SPLIT_RING, C, D], F32R)

        x_sb = sb("x_sb", [P, D])
        xn = sb("xn", [P, D])
        res = sb("res", [P, D])
        a_sb = sb("a_sb", [P, D])
        x1 = sb("x1", [P, D])
        xT_hi = sb("xT_hi", [P, C, P], F32R)
        xT_lo = sb("xT_lo", [P, C, P], F32R)
        xT = sb("xT", [P, C, P])
        row_sb = sb("row_sb", [P, len(ROWS), D])
        ln2_w_second = sb("ln2_w_second", [P, HALF])
        bias_raw = sb("bias_raw", [BK, D])
        bias_hl = sb("bias_hl", [BK, D], F32R)
        pick = sb("pick", [BK, NB, P], F32R)
        col_sb = sb("col_sb", [P, NCOL])
        ident = sb("ident", [P, P])
        iota = sb("iota", [P, P], BF16)
        ones = sb("ones", [P, P])
        zeros = sb("zeros", [P, HALF])
        count = sb("count", [P, P])
        count_i = sb("count_i", [P, P])
        ident_b = sb("ident_b", [P, P], BF16)
        mask = sb("mask", [P, P])
        deg = sb("deg", [P, P + 1])
        rdeg = sb("rdeg", [P, P])
        dinv = sb("dinv", [P, 1])
        dinv_diag = sb("dinv_diag", [P, P])
        dinv_row = sb("dinv_row", [P, P])
        mean_adj = sb("mean_adj", [P, P])
        gcn_adj = sb("gcn_adj", [P, P])
        gin_adj = sb("gin_adj", [P, GIN, P])
        eps_sb = sb("eps_sb", [P, GIN])
        minus_half = sb("minus_half", [P, 1])
        stat = sb("stat", [P, 7, 2, 6])
        mv = sb("mv", [P, 7, 2])
        rstd = sb("rstd", [P, 7])
        neg_max = sb("neg_max", [P, HEADS])
        rsum = sb("rsum", [P, HEADS])
        half_max = sb("half_max", [P, 2])
        minus_one = sb("minus_one", [P, 1])
        lsm = sb("lsm", [P, 4])

        with ExitStack() as attention:
            def tmp(name, shape, dt=F32):
                return attention.enter_context(nc.sbuf_tensor(name, shape, dt))

            edge_i = tmp("edge_i", [P, 2 * EC], I32)
            edge_f = tmp("edge_f", [P, 2 * EC])
            hot_src = tmp("hot_src", [P, EC, P], BF16)
            hot_dst = tmp("hot_dst", [P, EC, P], BF16)
            q_sb = tmp("q_sb", [P, D])
            k_sb = tmp("k_sb", [P, D])
            v_sb = tmp("v_sb", [P, HEADS, DH + 1])
            qT = tmp("qT", [P, C, P])
            kT = tmp("kT", [P, C, P])
            masked = tmp("masked", [P, HEADS, P])
            prob = tmp("prob", [P, HEADS, P])
            probT = tmp("probT", [P, HEADS, P])
            o_sb = tmp("o_sb", [P, D])
        up = sb("up", [P, 2, D])
        up_act = sb("up_act", [P, 2, C, P])
        upT_hi = sb("upT_hi", [P, FF // P, P], F32R)
        upT_lo = sb("upT_lo", [P, FF // P, P], F32R)
        nT_hi = sb("nT_hi", [P, C, P], F32R)
        nT_lo = sb("nT_lo", [P, C, P], F32R)
        h_sb = sb("h_sb", [P, D])

        x_in = sem("x_in")
        edges_in = sem("edges_in")
        cols_in = sem("cols_in")
        late_rows_in = sem("late_rows_in")
        bias_in = sem("bias_in")
        eps_in = sem("eps_in")
        w_in = {(g, p): sem(f"w_in_{g}{p}") for g in GROUPS for p in range(PIECES.get(g, 1))}
        out_done = sem("out_done")
        w_hi_ready = sem("w_hi_ready")
        w_lo_pool = sem("w_lo_pool")
        w_lo_dve = sem("w_lo_dve")
        bias_zero = sem("bias_zero")
        ln2_rows_full = sem("ln2_rows_full")
        ln2_w_ready = sem("ln2_w_ready")
        bias_hi_ready = sem("bias_hi_ready")
        bias_ready = sem("bias_ready")
        pick_ready = sem("pick_ready")
        pool_step = sem("pool_step")
        ident_ready = sem("ident_ready")
        iota_ready = sem("iota_ready")
        ident_b_ready = sem("ident_b_ready")
        ones_ready = sem("ones_ready")
        edges_ready = sem("edges_ready")
        src_ready = sem("src_ready")
        dst_ready = sem("dst_ready")
        pool_dst_ready = sem("pool_dst_ready")
        count_full = sem("count_full")
        count_ready = sem("count_ready")
        deg_full = sem("deg_full")
        deg_ready = sem("deg_ready")
        rdeg_ready = sem("rdeg_ready")
        mean_ready = sem("mean_ready")
        gin_adj_ready = sem("gin_adj_ready")
        gcn_adj_ready = sem("gcn_adj_ready")
        dve_step = sem("dve_step")
        var_ready = sem("var_ready")
        rstd_ready = sem("rstd_ready")
        normed = sem("normed")
        turned_full = [sem(f"turned_full{h}") for h in range(2)]
        turned_hi = [sem(f"turned_hi{h}") for h in range(2)]
        first_chunk_hi = sem("first_chunk_hi")
        first_chunk_whole = sem("first_chunk_whole")
        turned_out = [sem(f"turned_out{h}") for h in range(2)]
        rows_full = [sem(f"rows_full{h}") for h in range(2)]
        rows_out = [sem(f"rows_out{h}") for h in range(2)]
        neigh_full = sem("neigh_full")
        neigh_hi = [sem(f"neigh_hi{h}") for h in range(2)]
        neigh_out = [sem(f"neigh_out{h}") for h in range(2)]
        proj_full = sem("proj_full")
        q_rows = sem("q_rows")
        k_rows = sem("k_rows")
        v_ready = sem("v_ready")
        v_ones_ready = sem("v_ones_ready")
        scores_full = sem("scores_full")
        masked_ready = sem("masked_ready")
        prob_ready = sem("prob_ready")
        probT_full = sem("probT_full")
        probT_ready = sem("probT_ready")
        o_full = sem("o_full")
        o_ready = sem("o_ready")
        up_full = sem("up_full")
        up_rows = sem("up_rows")
        up_hi = sem("up_hi")
        down_used = sem("down_used")
        up_ready = sem("up_ready")
        diag_ready = sem("diag_ready")
        dinv_full = sem("dinv_full")
        dinv_row_ready = sem("dinv_row_ready")
        res_ready = sem("res_ready")
        max_ready = sem("max_ready")
        lse_ready = sem("lse_ready")
        shifted = sem("shifted")

        def hi(name):
            return w_hi[:, G[name] % SPLIT_RING]

        def lo(name):
            return w_lo[:, G[name] % SPLIT_RING]

        def raw_of(name):
            return raw[:, G[name] % RAW_RING]

        def loaded(name, c):
            return w_in[(name, c * PIECES.get(name, 1) // C)], 16

        def lo_made(name, c):
            on_pool = c in LO_ON_POOL[name]
            return (w_lo_pool if on_pool else w_lo_dve), lo_count(name, on_pool, c + 1)

        def two(t):
            return t[:, 0:HALF].rearrange("p (c n) -> p c n", c=2)

        def col(name, c):
            return col_sb[:, COL[name] + c:COL[name] + c + 1]

        def row(name, h=None):
            i = ROW[name]
            return row_sb[:, i, :] if h is None else row_sb[:, i, h * HALF:(h + 1) * HALF]

        def half(t, h):
            return t[:, h * HALF:(h + 1) * HALF]

        def chunk(t, c):
            return t[:, c * P:(c + 1) * P]

        group_used = {"q": (proj_full, 1), "k": (proj_full, 2), "v": (proj_full, 3), "out": (rows_full[1], R_OUT),
                      **{f"up{j}": (up_full, j + 1) for j in range(4)},
                      **{f"down{j}": (down_used, j + 1) for j in range(3)}, "down3": (rows_full[1], R_DOWN),
                      "self": (rows_full[1], R_L1), "neigh": (rows_full[1], R_L1),
                      **{f"gin{i}": (rows_full[1], R_GIN + i) for i in range(GIN)}}

        block = ctx.enter_context(nc.Block())

        @block.sync
        def _(sp):
            sp.dma_start(x_sb[:, :], x).then_inc(x_in, 16)
            for i, name in enumerate(GROUPS):
                if i >= RAW_RING:
                    before = GROUPS[i - RAW_RING]
                    sp.wait_ge(w_lo_pool, lo_count(before, True))
                    sp.wait_ge(w_lo_dve, lo_count(before, False))
                n = PIECES.get(name, 1)
                for p in range(n):
                    cs = slice(p * C // n, (p + 1) * C // n)
                    sp.dma_start(raw[:, i % RAW_RING, cs, :], weights[i, :, cs, :]).then_inc(w_in[(name, p)], 16)
                if name == "v":
                    sp.dma_start(eps_sb[:, :], eps.partition_broadcast(P)).then_inc(eps_in, 16)
                if name == "k":
                    sp.wait_ge(bias_zero, 1)
                    for at in (0, LO_AT):
                        sp.dma_start(bias_raw[at:at + NB, :], bias_rows).then_inc(bias_in, 16)
                if name == "self":
                    sp.dma_start(row_sb[:, :, :], rows.partition_broadcast(P)).then_inc(late_rows_in, 16)
            for h in range(2):
                sp.wait_ge(normed, 2 * 5 + h + 1)
                sp.dma_start(half(out, h), half(res, h)).then_inc(out_done, 16)
            sp.wait_ge(out_done, 32)

        @block.gpsimd
        def _(pool):
            done = [0]

            def link(ins):
                done[0] += 1
                ins.then_inc(pool_step, 1)
                pool.wait_ge(pool_step, done[0])

            def rsqrt_of_variance(i):
                pool.wait_ge(var_ready, i + 1)
                pool.tensor_tensor(rstd[:, i:i + 1], mv[:, i, 1:2], minus_half[:, :], ALU.pow)\
                    .then_inc(rstd_ready, 1)

            def split_lo(name, cs=range(C)):
                for c in (c for c in LO_ON_POOL[name] if c in cs):
                    pool.wait_ge(w_hi_ready, C * G[name] + c + 1)
                    pool.tensor_tensor(lo(name)[:, c, :], raw_of(name)[:, c, :], hi(name)[:, c, :].bitcast(F32),
                                       ALU.subtract).then_inc(w_lo_pool, 1)

            pool.memset(ones[:, :], 1.0).then_inc(ones_ready, 1)
            pool.memset(minus_half[:, :], -0.5)
            link(pool.memset(ident[:, :], 0.0))
            pool.affine_select(out=ident[:, :], in_=ident[:, :], compare_op=ALU.not_equal, fill=1.0, base=0,
                               pattern=[[-1, P]], channel_multiplier=1).then_inc(ident_ready, 1)
            pool.iota(iota[:, :], pattern=[[1, P]], base=0, channel_multiplier=0,
                      allow_small_or_imprecise_dtypes=True).then_inc(iota_ready, 1)
            pool.memset(bias_raw[:, :], 0.0).then_inc(bias_zero, 1)
            pool.memset(v_sb[:, :, DH:], 1.0).then_inc(v_ones_ready, 1)
            rsqrt_of_variance(LN1)
            split_lo("q")

            pool.wait_ge(edges_ready, 1)
            pool.wait_ge(iota_ready, 1)
            for e in range(EC - DST_ON_POOL, EC):
                pool.tensor_scalar(hot_dst[:, e, :], iota[:, :], edge_f[:, EC + e:EC + e + 1], None,
                                   ALU.is_equal).then_inc(pool_dst_ready, 1)
            split_lo("k")
            pool.wait_ge(bias_hi_ready, 1)
            pool.wait_ge(w_lo_pool, lo_count("k", True))
            pool.tensor_tensor(bias_hl[LO_AT:, :], bias_raw[LO_AT:, :], bias_hl[LO_AT:, :].bitcast(F32), ALU.subtract)\
                .then_inc(bias_ready, 1)
            pool.wait_ge(bias_ready, 1)
            split_lo("v")
            split_lo("out")
            split_lo("up0")
            rsqrt_of_variance(LN2)
            split_lo("up1")
            pool.wait_ge(deg_ready, 1)
            link(pool.tensor_tensor(dinv[:, :], deg[:, P:P + 1], minus_half[:, :], ALU.pow))
            pool.wait_ge(ident_ready, 1)
            pool.tensor_scalar(dinv_diag[:, :], ident[:, :], dinv[:, :], None, ALU.mult).then_inc(diag_ready, 1)
            split_lo("up2")
            split_lo("up3")
            split_lo("down0")
            for h in range(2):
                pool.wait_ge(rows_out[h], R_OUT)
            pool.tensor_tensor(res[:, :], x_sb[:, :], a_sb[:, :], ALU.add).then_inc(res_ready, 1)
            split_lo("down1")
            pool.wait_ge(eps_in, 16)
            link(pool.tensor_tensor(gin_adj[:, :, :], ident[:, :].unsqueeze(1).broadcast_to([P, GIN, P]),
                                    eps_sb[:, :].unsqueeze(2).broadcast_to([P, GIN, P]), ALU.mult))
            split_lo("down2")
            pool.wait_ge(count_ready, 1)
            pool.tensor_tensor(gin_adj[:, :, :], gin_adj[:, :, :],
                               count_i[:, :].unsqueeze(1).broadcast_to([P, GIN, P]), ALU.add)\
                .then_inc(gin_adj_ready, 1)
            split_lo("down3")
            link(pool.tensor_tensor(count[:, :], count_i[:, :], ident[:, :], ALU.subtract))
            pool.wait_ge(rdeg_ready, 1)
            pool.tensor_tensor(mean_adj[:, :], count[:, :], rdeg[:, :], ALU.mult).then_inc(mean_ready, 1)
            split_lo("self")
            rsqrt_of_variance(LNX1)
            split_lo("neigh")
            pool.wait_ge(late_rows_in, 16)
            pool.wait_ge(normed, 2 * 2 + 2)
            pool.tensor_tensor(res[:, :], x1[:, :], row("beta"), ALU.add).then_inc(res_ready, 1)
            split_lo("gin0")
            split_lo("gin1")
            rsqrt_of_variance(LNH)
            rsqrt_of_variance(LNX2)
            split_lo("gin2")
            split_lo("gin3")
            link(pool.tensor_scalar(gcn_adj[:, :], count_i[:, :], dinv[:, :], None, ALU.mult))
            pool.wait_ge(dinv_row_ready, 1)
            pool.tensor_tensor(gcn_adj[:, :], gcn_adj[:, :], dinv_row[:, :], ALU.mult).then_inc(gcn_adj_ready, 1)
            split_lo("gin4")
            split_lo("gcn")
            split_lo("dense")
            rsqrt_of_variance(LNX3)
            pool.wait_ge(normed, 2 * 4 + 2)
            pool.tensor_tensor(res[:, :], xn[:, :], row("b_dense"), ALU.add).then_inc(res_ready, 1)
            rsqrt_of_variance(LNX4)

        @block.scalar
        def _(act):
            act.dma_start(edge_i[:, :], edges).then_inc(edges_in, 16)
            act.dma_start(col_sb[:, :], cols).then_inc(cols_in, 16)
            act.preload_act_table_set("natural_log_exp_and_others")

            def split_hi(name, cs):
                i = G[name]
                if cs[0] == 0 and i >= SPLIT_RING:
                    act.wait_ge(*group_used[GROUPS[i - SPLIT_RING]])
                act.wait_ge(*loaded(name, cs[-1]))
                lo_c, hi_c = cs[0], cs[-1] + 1
                act.activation(hi(name)[:, lo_c:hi_c, :], raw_of(name)[:, lo_c:hi_c, :], ACT.Copy)\
                    .then_inc(w_hi_ready, len(cs))

            def split_hi_group(name):
                split_hi(name, [0, 1])
                split_hi(name, [2, 3])

            def turned_hi_parts(n, halves=range(2)):
                for h in halves:
                    act.wait_ge(turned_full[h], n)
                    act.activation(xT_hi[:, 2 * h:2 * h + 2, :], two(T[h]), ACT.Copy).then_inc(turned_hi[h], 1)

            def ln1_chunk(dst, c, ready):
                act.activation(dst, chunk(T[0], c), ACT.Identity, bias=col("ln1_b", c), scale=col("ln1_w", c))\
                    .then_inc(ready, 1)

            def heads_turned(n, dst, bias, banks):
                act.wait_ge(turned_full[0], n)
                for c in range(2):
                    ins = act.activation(dst[:, c, :], chunk(banks[0], c), ACT.Identity, bias=bias(c))
                ins.then_inc(turned_out[0], 1)

            split_hi("q", [0])
            split_hi("q", [1])
            split_hi("q", [2])
            act.wait_ge(cols_in, 16)
            act.wait_ge(turned_full[0], T_LN1)
            ln1_chunk(xT_hi[:, 0, :], 0, first_chunk_hi)
            ln1_chunk(xT_hi[:, 1, :], 1, turned_hi[0])
            split_hi("q", [3])
            ln1_chunk(xT[:, 0, :], 0, first_chunk_whole)
            split_hi_group("k")
            act.wait_ge(bias_in, 32)
            act.activation(bias_hl[:, :], bias_raw[:, :], ACT.Copy).then_inc(bias_hi_ready, 1)
            act.wait_ge(proj_full, 1)
            act.activation(q_sb[:, :], U[0][:, :], ACT.Copy).then_inc(q_rows, 1)
            split_hi("v", [0, 1])
            act.wait_ge(proj_full, 2)
            act.activation(k_sb[:, :], U[1][:, :], ACT.Copy).then_inc(k_rows, 1)
            heads_turned(T_Q, qT, lambda c: col("b_q", c), T)
            heads_turned(T_K, kT, lambda c: col("b_k", c), K_TURNED)
            split_hi("v", [2, 3])
            split_hi_group("out")
            for i, h in enumerate(HEAD_ORDER):
                act.wait_ge(masked_ready, i + 1)
                act.activation(prob[:, h, :], masked[:, h, :], ACT.Exp, bias=neg_max[:, h:h + 1], scale=-1.0)\
                    .then_inc(prob_ready, 1)
            split_hi_group("up0")
            split_hi("up1", [0, 1])
            turned_hi_parts(T_O, halves=[1])
            split_hi("up1", [2, 3])
            act.wait_ge(ln2_rows_full, 1)
            act.activation(ln2_w_second[:, :], half(U[2], 1), ACT.Copy).then_inc(ln2_w_ready, 1)
            split_hi_group("up2")
            turned_hi_parts(T_LN2, halves=[1])
            split_hi_group("up3")

            def up_to_sbuf(j):
                act.wait_ge(up_full, j + 1)
                if j >= 2:
                    act.wait_ge(turned_full[1], T_UP + j - 2)
                act.activation(up[:, j % 2, :], U[j][:, :], ACT.Copy).then_inc(up_rows, 1)

            def up_turned(j):
                act.wait_ge(turned_full[0], T_UP + j)
                if j >= 2:
                    act.wait_ge(up_ready, j - 1)
                for c in range(2):
                    ins = act.activation(up_act[:, j % 2, c, :], chunk(T[0], c), ACT.Relu, bias=col("b_up", C * j + c))
                ins.then_inc(turned_out[0], 1)

            def rows_to_h(r, function):
                for h in range(2):
                    act.wait_ge(rows_full[h], r)
                    act.activation(half(h_sb, h), R[h][:, 0:HALF], function).then_inc(rows_out[h], 1)

            up_to_sbuf(0)
            split_hi_group("down0")
            up_to_sbuf(1)
            up_turned(0)
            split_hi_group("down1")
            up_to_sbuf(2)
            up_turned(1)
            split_hi_group("down2")
            up_to_sbuf(3)
            up_turned(2)
            split_hi_group("down3")
            up_turned(3)
            split_hi_group("self")
            split_hi_group("neigh")
            turned_hi_parts(T_X1)
            for h in range(2):
                act.wait_ge(neigh_full, h + 1)
                act.activation(nT_hi[:, 2 * h:2 * h + 2, :], two(U[h]), ACT.Copy).then_inc(neigh_hi[h], 1)
            split_hi_group("gin0")
            split_hi_group("gin1")
            split_hi_group("gin2")
            for i in range(GIN):
                turned_hi_parts(T_GIN + i)
                if i < 4:
                    split_hi_group(["gin3", "gin4", "gcn", "dense"][i])
                if i < GIN - 1:
                    rows_to_h(R_GIN + i, ACT.Relu)
            for h in range(2):
                act.wait_ge(rows_out[h], R_GIN + GIN - 1)
                act.activation(half(a_sb, h), half(h_sb, h), ACT.Relu).then_inc(lse_ready, 1)
            act.wait_ge(max_ready, 1)
            act.wait_ge(lse_ready, 2)
            act.activation(a_sb[:, :], a_sb[:, :], ACT.Exp, bias=lsm[:, 0:1], accum_out=lsm[:, 1:2])\
                .then_inc(lse_ready, 1)
            act.wait_ge(lse_ready, 3)
            act.activation(lsm[:, 2:3], lsm[:, 1:2], ACT.Ln).then_inc(lse_ready, 1)
            act.wait_ge(lse_ready, 4)
            act.activation(lsm[:, 3:4], lsm[:, 2:3], ACT.Identity, bias=lsm[:, 0:1], scale=-1.0)\
                .then_inc(lse_ready, 1)
            act.wait_ge(lse_ready, 5)
            act.wait_ge(var_ready, LNX3 + 1)
            act.activation(half(xn, 1), half(xn, 1), ACT.Identity, bias=lsm[:, 3:4]).then_inc(shifted, 1)
            turned_hi_parts(T_X3)
            rows_to_h(R_GCN, ACT.Copy)
            turned_hi_parts(T_AGG)

        @block.tensor
        def _(pe):
            def turn(n, src, ready, first, between=None):
                for h in range(2):
                    pe.wait_ge(ready, first + h)
                    if n > 1:
                        pe.wait_ge(turned_out[h], n - 1)
                    for c in range(2):
                        ins = pe.transpose(chunk(T[h], c), chunk(src, 2 * h + c), ident[:, :])
                    ins.then_inc(turned_full[h], 1)
                    if h == 0 and between is not None:
                        between()

            def aggregate(n, src, adj, ready, first, bias=None, then=None):
                for h in range(2):
                    pe.wait_ge(turned_out[h], n - 1)
                    for c in range(2):
                        if bias is not None:
                            pe.matmul(chunk(T[h], c), bias_raw[0:NB, (2 * h + c) * P:(2 * h + c + 1) * P],
                                      pick[0:NB, BIAS.index(bias), :].bitcast(F32), start=True, stop=False)
                        if c == 0:
                            pe.wait_ge(ready[h], first[h])
                        ins = pe.matmul(chunk(T[h], c), chunk(src, 2 * h + c), adj, start=bias is None, stop=True)
                    ins.then_inc(turned_full[h], 1)
                    if then is not None:
                        then(h)

            def weights_there(name, c):
                pe.wait_ge(w_hi_ready, C * G[name] + c + 1)
                pe.wait_ge(*lo_made(name, c))

            def product(out, name, cols, x_hi, x_lo, start=True, stop=True, hi_there=None, lo_there=None):
                for c in range(C):
                    if hi_there is not None:
                        hi_there(c)
                        weights_there(name, c)
                    pe.matmul(out, x_hi[:, c, :], hi(name)[:, c, cols], start=(start and c == 0), stop=False)
                    pe.matmul(out, x_hi[:, c, :], lo(name)[:, c, cols], start=False, stop=False)
                for c in range(C):
                    if lo_there is not None:
                        lo_there(c)
                    ins = pe.matmul(out, x_lo[:, c, :], hi(name)[:, c, cols], start=False, stop=(stop and c == C - 1))
                return ins

            def turned_there(n):
                def hi_there(c):
                    if c % 2 == 0:
                        pe.wait_ge(turned_hi[c // 2], HI_FILLS.index(n) + 1)

                def lo_there(c):
                    if c % 2 == 0:
                        pe.wait_ge(turned_out[c // 2], n)
                return hi_there, lo_there

            def spread_row(dst, name, cols, start=True, stop=False):
                return pe.matmul(dst, pick[:, BIAS.index(name), :], bias_hl[:, cols], start=start, stop=stop)

            def bias_row(name, r, h):
                if r > 1:
                    pe.wait_ge(rows_out[h], r - 1)
                spread_row(R[h][:, 0:HALF], name, slice(h * HALF, (h + 1) * HALF))

            def row_halves(name, x_hi, x_lo, order, there, r=None, start=(), full=True, into=R):
                hi_there, lo_there = there
                seen_hi, seen_lo = set(), set()
                for h, cs in order:
                    if h in start and cs[0] == 0 and r > 1:
                        pe.wait_ge(rows_out[h], r - 1)
                    at = slice(h * HALF, (h + 1) * HALF)
                    for c in cs:
                        if c not in seen_hi:
                            seen_hi.add(c)
                            hi_there(c)
                            weights_there(name, c)
                        pe.matmul(into[h][:, 0:HALF], x_hi[:, c, :], hi(name)[:, c, at],
                                  start=h in start and c == 0, stop=False)
                        pe.matmul(into[h][:, 0:HALF], x_hi[:, c, :], lo(name)[:, c, at], start=False, stop=False)
                    for c in cs:
                        if c not in seen_lo:
                            seen_lo.add(c)
                            lo_there(c)
                        ins = pe.matmul(into[h][:, 0:HALF], x_lo[:, c, :], hi(name)[:, c, at], start=False,
                                        stop=full and c == C - 1)
                    if full and cs[-1] == C - 1:
                        ins.then_inc(rows_full[h], 1)

            EVEN = [(0, (0, 1)), (1, (0, 1)), (0, (2, 3)), (1, (2, 3))]
            APART = [(0, (0, 1)), (1, (0,)), (0, (2, 3)), (1, (1, 2, 3))]

            def project(i, name, cs):
                for c in cs:
                    if i == 0:
                        pe.wait_ge([first_chunk_hi, turned_hi[0], turned_hi[1], turned_hi[1]][c], 1)
                    pe.wait_ge(w_hi_ready, C * G[name] + c + 1)
                    pe.matmul(U[i][:, :], xT_hi[:, c, :], hi(name)[:, c, :], start=(c == 0), stop=False)

            def project_x_lo(i, name, cs):
                for c in cs:
                    if i == 0:
                        pe.wait_ge(turned_out[c // 2], T_LN1)
                    pe.matmul(U[i][:, :], xT_lo[:, c, :], hi(name)[:, c, :], start=False, stop=False)

            def project_w_lo(i, name, cs):
                for c in cs:
                    pe.wait_ge(*lo_made(name, c))
                    ins = pe.matmul(U[i][:, :], xT_hi[:, c, :], lo(name)[:, c, :], start=False,
                                    stop=(c == C - 1))
                return ins

            def keep_warm(n):
                for _ in range(n):
                    pe.matmul(T[0][:, HALF:HALF + P], ones[:, :], ones[:, :], start=True, stop=True)

            def turn_rows(src, ready, banks):
                pe.wait_ge(ready, 1)
                for h in range(2):
                    if banks is T:
                        pe.wait_ge(turned_out[h], T_LN1)
                    for c in range(2):
                        ins = pe.transpose(chunk(banks[h], c), chunk(src, 2 * h + c), ident[:, :])
                    ins.then_inc(turned_full[h], 1)

            pe.wait_ge(ones_ready, 1)
            keep_warm(WARM["start"])
            pe.wait_ge(ident_ready, 1)
            turn(T_LN1, xn, normed, 1)
            for c in range(2):
                project(0, "q", [c])
                project_w_lo(0, "q", [c])
            project(0, "q", range(2, C))
            project_x_lo(0, "q", [2, 3, 0, 1])
            project(1, "k", range(0, 2))
            project_x_lo(1, "k", range(0, 2))
            project_w_lo(0, "q", range(2, C)).then_inc(proj_full, 1)
            project(1, "k", range(2, C))
            project_x_lo(1, "k", range(2, C))
            project_w_lo(1, "k", range(C)).then_inc(proj_full, 1)
            turn_rows(q_sb, q_rows, T)
            project(2, "v", range(0, 2))
            turn_rows(k_sb, k_rows, K_TURNED)
            project_x_lo(2, "v", range(0, 2))

            def count_edges(es):
                for e in es:
                    pe.wait_ge(src_ready, e + 1)
                    if e < EC - DST_ON_POOL:
                        pe.wait_ge(dst_ready, e + 1)
                    else:
                        pe.wait_ge(pool_dst_ready, e - (EC - DST_ON_POOL) + 1)
                    ins = pe.matmul(U[3][:, 0:P], hot_src[:, e, :], hot_dst[:, e, :], start=False, stop=(e == EC - 1))
                return ins

            pe.wait_ge(ident_b_ready, 1)
            pe.matmul(U[3][:, 0:P], ident_b[:, :], ident_b[:, :], start=True, stop=False)
            score_bank = [R[0], R[1], U[0], U[1]]
            for h in range(HEADS):
                if h % 4 == 0:
                    pe.wait_ge(turned_out[h // 4], T_K)
                at_row = (h % 2) * DH
                b = score_bank[2 * (h // 4) + h % 2]
                at = (h % 4) // 2
                ins = pe.matmul(b[:, at * P:(at + 1) * P], qT[at_row:at_row + DH, h // 2, :],
                                kT[at_row:at_row + DH, h // 2, :], start=True, stop=True)
                if h % 4 >= 2:
                    ins.then_inc(scores_full, 1)
            count_edges(range(EC)).then_inc(count_full, 1)
            project(2, "v", range(2, C))
            project_x_lo(2, "v", range(2, C))
            pe.wait_ge(count_ready, 1)
            pe.wait_ge(ones_ready, 1)
            pe.matmul(U[3][:, 0:P], ones[:, :], count_i[:, :], start=True, stop=True)
            pe.matmul(U[3][:, P:P + 1], count_i[:, :], ones[:, 0:1], start=True, stop=True).then_inc(deg_full, 1)
            pe.wait_ge(bias_ready, 1)
            pe.wait_ge(pick_ready, 2)
            spread_row(U[2][:, :], "v", slice(0, D), start=False)
            project_w_lo(2, "v", range(C)).then_inc(proj_full, 1)

            prob_bank = [R[0], R[1], U[3], T[0]]

            def turn_prob(i):
                if i == 2:
                    pe.wait_ge(deg_ready, 1)
                pe.wait_ge(prob_ready, 2 * i + 2)
                for k in range(2):
                    ins = pe.transpose(chunk(prob_bank[i], k), prob[:, HEAD_ORDER[2 * i + k], :], ident[:, :])
                ins.then_inc(probT_full, 1)

            def attend(i):
                pe.wait_ge(probT_ready, i + 1)
                for h in HEAD_ORDER[2 * i:2 * i + 2]:
                    at = (h % 4) * (DH + 1)
                    ins = pe.matmul(U[h // 4][:, at:at + DH + 1], probT[:, h, :], v_sb[:, h, :], start=True, stop=True)
                if i % 2:
                    ins.then_inc(o_full, 1)

            turn_prob(0)
            turn_prob(1)
            turn_prob(2)
            turn_prob(3)
            pe.wait_ge(v_ready, 1)
            pe.wait_ge(v_ones_ready, 1)
            attend(0)
            attend(1)
            attend(2)
            attend(3)
            bias_row("out", R_OUT, 0)

            def residual_of_attention():
                bias_row("out", R_OUT, 1)
                pe.matmul(R[1][:, 0:HALF], ident[:, :], half(x_sb, 1), start=False, stop=False)
            turn(T_O, o_sb, o_ready, 1, between=residual_of_attention)
            row_halves("out", xT_hi, xT_lo, APART, turned_there(T_O))
            for dst, name in [(U[2], "ln2_w"), (U[3], "ln2_b")]:
                spread_row(dst[:, :], name, slice(0, D), stop=True).then_inc(ln2_rows_full, 1)
            keep_warm(WARM["ln2"])
            turn(T_LN2, xn, normed, 3)

            def up_block(j):
                hi_there, lo_there = turned_there(T_LN2)
                product(U[j][:, :], f"up{j}", slice(0, D), xT_hi, xT_lo, hi_there=hi_there, lo_there=lo_there)\
                    .then_inc(up_full, 1)

            def turn_up(j):
                pe.wait_ge(up_rows, j + 1)
                if j == 0:
                    pe.wait_ge(dinv_row_ready, 1)
                for h in range(2):
                    pe.wait_ge(turned_out[h], T_UP + j - 1)
                    for c in range(2):
                        ins = pe.transpose(chunk(T[h], c), chunk(up[:, j % 2], 2 * h + c), ident[:, :])
                    ins.then_inc(turned_full[h], 1)

            def down_block(j):
                def hi_there(c):
                    if c == 0:
                        pe.wait_ge(up_hi, j + 1)

                def lo_there(c):
                    if c == 0:
                        pe.wait_ge(up_ready, j + 1)
                for h in range(2):
                    if j == 0:
                        bias_row("down", R_DOWN, h)
                    ins = product(R[h][:, 0:HALF], f"down{j}", slice(h * HALF, (h + 1) * HALF),
                                  upT_hi[:, C * j:C * j + C, :], upT_lo[:, C * j:C * j + C, :],
                                  start=False, stop=(j == 3), hi_there=hi_there if h == 0 else None,
                                  lo_there=lo_there if h == 0 else None)
                    if j == 3:
                        ins.then_inc(rows_full[h], 1)
                if j < 3:
                    ins.then_inc(down_used, 1)

            up_block(0)
            pe.wait_ge(diag_ready, 1)
            pe.wait_ge(turned_out[1], T_LN2)
            pe.matmul(T[1][:, HALF:HALF + P], ones[:, :], dinv_diag[:, :], start=True, stop=True).then_inc(dinv_full, 1)
            up_block(1)
            turn_up(0)
            up_block(2)
            turn_up(1)
            up_block(3)
            turn_up(2)
            down_block(0)
            turn_up(3)
            down_block(1)
            down_block(2)
            down_block(3)

            keep_warm(WARM["x1"])
            for h in range(2):
                bias_row("l1", R_L1, h)
            turn(T_X1, x1, normed, 5)
            pe.wait_ge(mean_ready, 1)
            for h in range(2):
                for c in range(2):
                    ins = pe.matmul(chunk(U[h], c), chunk(x1, 2 * h + c), mean_adj[:, :], start=True, stop=True)
                ins.then_inc(neigh_full, 1)
            row_halves("self", xT_hi, xT_lo, EVEN, turned_there(T_X1), full=False)

            def neigh_hi_there(c):
                if c % 2 == 0:
                    pe.wait_ge(neigh_hi[c // 2], 1)

            def neigh_lo_there(c):
                if c % 2 == 0:
                    pe.wait_ge(neigh_out[c // 2], 1)
            row_halves("neigh", nT_hi, nT_lo, APART, (neigh_hi_there, neigh_lo_there))

            keep_warm(WARM["x2"])
            pe.wait_ge(gin_adj_ready, 1)
            for i in range(GIN):
                src, ready, first = (xn, [normed, normed], [7, 8]) if i == 0 else (h_sb, rows_out, [R_GIN + i - 1] * 2)
                aggregate(T_GIN + i, src, gin_adj[:, i, :], ready, first,
                          then=lambda h: bias_row(f"gin{i}", R_GIN + i, h))
                row_halves(f"gin{i}", xT_hi, xT_lo, EVEN if i < GIN - 1 else APART, turned_there(T_GIN + i))

            keep_warm(WARM["x3"])
            turn(T_X3, xn, normed, 9)
            pe.matmul(U[1][:, 0:HALF], pick[:, BIAS.index("dense"), :], half(bias_hl, 1), start=True, stop=False)
            pe.matmul(U[1][:, 0:HALF], ident[:, :], half(xn, 1), start=False, stop=False)
            row_halves("gcn", xT_hi, xT_lo, EVEN, turned_there(T_X3), r=R_GCN, start=[0, 1])
            pe.wait_ge(gcn_adj_ready, 1)
            aggregate(T_AGG, h_sb, gcn_adj[:, :], rows_out, [R_GCN] * 2, bias="gcn")
            row_halves("dense", xT_hi, xT_lo, APART, turned_there(T_AGG), r=R_DENSE, start=[0], into=U)

        @block.vector
        def _(dve):
            done = [0]
            first_half = [0]

            def mark(ins):
                done[0] += 1
                ins.then_inc(dve_step, 1)

            def link(ins):
                mark(ins)
                dve.wait_ge(dve_step, done[0])

            def stats(i, h, src):
                mark(dve.bn_stats(stat[:, i, h, :], src))
                if h == 0:
                    first_half[0] = done[0]

            def take_epsilon(i):
                dve.wait_ge(dve_step, first_half[0])
                mark(dve.tensor_scalar(stat[:, i, 0, 2:3], stat[:, i, 0, 2:3], LN_EPS * D, None, ALU.add))

            def mean_and_variance(i):
                dve.wait_ge(dve_step, done[0])
                dve.bn_aggr(mv[:, i, :], stat[:, i, :, :].rearrange("p a b -> p (a b)")).then_inc(var_ready, 1)
                dve.wait_ge(var_ready, i + 1)

            def mean_and_rstd(i):
                mean_and_variance(i)
                dve.wait_ge(rstd_ready, i + 1)

            def apply(i, src, dst, before_second=None):
                for h in range(2):
                    if h == 1 and before_second is not None:
                        dve.wait_ge(*before_second)
                    dve.tensor_scalar(half(dst, h), src[h], mv[:, i, 0:1], rstd[:, i:i + 1],
                                      ALU.subtract, ALU.mult).then_inc(normed, 1)

            def split_lo(name, cs=range(C)):
                for c in cs:
                    if c not in LO_ON_POOL[name]:
                        dve.wait_ge(w_hi_ready, C * G[name] + c + 1)
                        dve.tensor_tensor(lo(name)[:, c, :], raw_of(name)[:, c, :], hi(name)[:, c, :].bitcast(F32),
                                          ALU.subtract).then_inc(w_lo_dve, 1)

            def turned_lo_parts(n, first_hi=False, between=None):
                if first_hi:
                    dve.wait_ge(turned_full[0], n)
                    dve.tensor_copy(xT_hi[:, 0:2, :], two(T[0])).then_inc(turned_hi[0], 1)
                for h in range(2):
                    dve.wait_ge(turned_full[h], n)
                    dve.wait_ge(turned_hi[h], HI_FILLS.index(n) + 1)
                    dve.tensor_tensor(xT_lo[:, 2 * h:2 * h + 2, :], two(T[h]),
                                      xT_hi[:, 2 * h:2 * h + 2, :].bitcast(F32), ALU.subtract)\
                        .then_inc(turned_out[h], 1)
                    if h == 0 and between is not None:
                        between()

            def turned_ln1_parts():
                for h, cs in [(1, [2, 3]), (0, [1])]:
                    pair = slice(2 * h, 2 * h + 2)
                    dve.wait_ge(turned_full[h], T_LN1)
                    if h == 0:
                        dve.wait_ge(turned_hi[0], 1)
                        dve.wait_ge(first_chunk_whole, 1)
                    for c in cs:
                        mark(dve.tensor_scalar(xT[:, c, :], chunk(T[h], c % 2), col("ln1_w", c), col("ln1_b", c),
                                               ALU.mult, ALU.add))
                    dve.wait_ge(dve_step, done[0])
                    if h == 1:
                        dve.tensor_copy(xT_hi[:, pair, :], xT[:, pair, :]).then_inc(turned_hi[1], 1)
                        dve.wait_ge(turned_hi[1], 1)
                    dve.tensor_tensor(xT_lo[:, pair, :], xT[:, pair, :], xT_hi[:, pair, :].bitcast(F32),
                                      ALU.subtract).then_inc(turned_out[h], 1)

            def heads_turned(n, dst, bias, banks):
                dve.wait_ge(turned_full[1], n)
                for c in range(2, 4):
                    ins = dve.tensor_scalar(dst[:, c, :], chunk(banks[1], c - 2), bias(c), None, ALU.add)
                ins.then_inc(turned_out[1], 1)

            mark(dve.memset(zeros[:, :], 0.0))
            mark(dve.memset(minus_one[:, :], -1.0))
            dve.wait_ge(ident_ready, 1)
            dve.tensor_copy(ident_b[:, :], ident[:, :]).then_inc(ident_b_ready, 1)

            def picks(first, last):
                shape = [BK, last - first, P]
                dve.tensor_tensor(pick[:, first:last, :], ident[0:BK, first:last].unsqueeze(2).broadcast_to(shape),
                                  ident[0:BK, LO_AT + first:LO_AT + last].unsqueeze(2).broadcast_to(shape), ALU.add)\
                    .then_inc(pick_ready, 1)
            picks(0, NB - 4)
            dve.wait_ge(x_in, 16)
            for h in range(2):
                stats(LN1, h, half(x_sb, h))
            take_epsilon(LN1)
            mean_and_variance(LN1)
            picks(NB - 4, NB)
            dve.wait_ge(rstd_ready, LN1 + 1)
            apply(LN1, [half(x_sb, 0), half(x_sb, 1)], xn)
            dve.wait_ge(edges_in, 16)
            dve.tensor_copy(edge_f[:, :], edge_i[:, :]).then_inc(edges_ready, 1)
            dve.wait_ge(edges_ready, 1)
            dve.wait_ge(iota_ready, 1)

            def one_hot(dst, at, es, ready):
                for e in es:
                    dve.tensor_scalar(dst[:, e, :], iota[:, :], edge_f[:, at + e:at + e + 1], None,
                                      ALU.is_equal).then_inc(ready, 1)
            one_hot(hot_src, 0, range(0, 4), src_ready)
            dve.wait_ge(cols_in, 16)
            turned_ln1_parts()
            split_lo("q")
            split_lo("k")
            one_hot(hot_src, 0, range(4, 14), src_ready)
            heads_turned(T_Q, qT, lambda c: col("b_q", c), T)
            one_hot(hot_src, 0, range(14, EC), src_ready)
            heads_turned(T_K, kT, lambda c: col("b_k", c), K_TURNED)
            one_hot(hot_dst, EC, range(0, EC - DST_ON_POOL), dst_ready)
            split_lo("v")
            dve.wait_ge(count_full, 1)
            mark(dve.tensor_scalar(mask[:, :], U[3][:, 0:P], 0.0, -NEG * DH ** 0.5, ALU.is_equal, ALU.mult))
            dve.tensor_copy(count_i[:, :], U[3][:, 0:P]).then_inc(count_ready, 1)
            dve.wait_ge(dve_step, done[0])
            score_bank = [R[0], R[1], U[0], U[1]]
            for i, h in enumerate(HEAD_ORDER):
                if i % 2 == 0:
                    dve.wait_ge(scores_full, i // 2 + 1)
                if i == 6:
                    dve.wait_ge(deg_full, 1)
                    dve.tensor_copy(deg[:, :], U[3][:, 0:P + 1]).then_inc(deg_ready, 1)
                dve.tensor_tensor_reduce(masked[:, h, :], chunk(score_bank[i // 2], i % 2), mask[:, :],
                                         -(DH ** -0.5), 3.0e38, ALU.add, ALU.min,
                                         neg_max[:, h:h + 1]).then_inc(masked_ready, 1)
            prob_bank = [R[0], R[1], U[3], T[0]]

            def probT_to_sbuf(i):
                dve.wait_ge(probT_full, i + 1)
                h = HEAD_ORDER[2 * i]
                dve.tensor_copy(probT[:, h:h + 3:2, :], two(prob_bank[i])).then_inc(probT_ready, 1)

            def normalise_o(g):
                dve.wait_ge(o_full, g + 1)
                heads = U[g][:, 0:4 * (DH + 1)].rearrange("p (h d) -> p h d", h=4)
                link(dve.reciprocal(rsum[:, 4 * g:4 * g + 4], heads[:, :, DH]))
                dve.tensor_tensor(half(o_sb, g).rearrange("p (h d) -> p h d", h=4), heads[:, :, 0:DH],
                                  rsum[:, 4 * g:4 * g + 4].unsqueeze(2).broadcast_to([P, 4, DH]),
                                  ALU.mult).then_inc(o_ready, 1)

            dve.wait_ge(proj_full, 3)
            dve.tensor_copy(v_sb[:, :, 0:DH], U[2][:, :].rearrange("p (h d) -> p h d", h=HEADS)).then_inc(v_ready, 1)
            probT_to_sbuf(0)
            probT_to_sbuf(1)
            probT_to_sbuf(2)
            probT_to_sbuf(3)
            normalise_o(0)
            normalise_o(1)
            turned_lo_parts(T_O, first_hi=True, between=lambda: split_lo("out"))
            split_lo("up0")
            dve.wait_ge(rows_full[0], R_OUT)
            dve.tensor_tensor(half(a_sb, 0), R[0][:, 0:HALF], half(x_sb, 0), ALU.add).then_inc(rows_out[0], 1)
            dve.wait_ge(rows_out[0], R_OUT)
            stats(LN2, 0, half(a_sb, 0))
            dve.wait_ge(rows_full[1], R_OUT)
            stats(LN2, 1, R[1][:, 0:HALF])
            take_epsilon(LN2)
            mean_and_variance(LN2)
            dve.wait_ge(ln2_rows_full, 2)
            dve.wait_ge(ln2_w_ready, 1)
            halves = [(half(a_sb, 0), half(U[2], 0)), (R[1][:, 0:HALF], ln2_w_second[:, :])]
            for h, (a_half, w_half) in enumerate(halves):
                mark(dve.scalar_tensor_tensor(half(xn, h), a_half, mv[:, LN2, 0:1], w_half,
                                              ALU.subtract, ALU.mult))
            dve.wait_ge(dve_step, done[0])
            dve.wait_ge(rstd_ready, LN2 + 1)
            for h in range(2):
                dve.scalar_tensor_tensor(half(xn, h), half(xn, h), rstd[:, LN2:LN2 + 1], half(U[3], h),
                                         ALU.mult, ALU.add).then_inc(normed, 1)
            turned_lo_parts(T_LN2, first_hi=True)
            split_lo("up1")
            dve.tensor_copy(half(a_sb, 1), R[1][:, 0:HALF]).then_inc(rows_out[1], 1)
            dve.wait_ge(dinv_full, 1)
            dve.tensor_copy(dinv_row[:, :], T[1][:, HALF:HALF + P]).then_inc(dinv_row_ready, 1)
            split_lo("up2")
            split_lo("up3")
            link(dve.tensor_scalar(rdeg[:, :], deg[:, 0:P], 1.0, 1.0, ALU.subtract, ALU.max))
            dve.reciprocal(rdeg[:, :], rdeg[:, :]).then_inc(rdeg_ready, 1)
            split_lo("down0")

            def up_turned(j):
                dve.wait_ge(turned_full[1], T_UP + j)
                for c in range(2, C):
                    ins = dve.tensor_scalar(up_act[:, j % 2, c, :], chunk(T[1], c - 2), col("b_up", C * j + c), 0.0,
                                            ALU.add, ALU.max)
                ins.then_inc(turned_out[1], 1)
                for h in range(2):
                    dve.wait_ge(turned_out[h], T_UP + j)
                block_hi, block_lo = upT_hi[:, C * j:C * j + C, :], upT_lo[:, C * j:C * j + C, :]
                dve.tensor_copy(block_hi, up_act[:, j % 2, :, :]).then_inc(up_hi, 1)
                dve.wait_ge(up_hi, j + 1)
                dve.tensor_tensor(block_lo, up_act[:, j % 2, :, :], block_hi.bitcast(F32), ALU.subtract)\
                    .then_inc(up_ready, 1)

            up_turned(0)
            split_lo("down1")
            up_turned(1)
            split_lo("down2")
            up_turned(2)
            split_lo("down3")
            up_turned(3)
            split_lo("self")
            dve.wait_ge(res_ready, 1)
            for h in range(2):
                dve.wait_ge(rows_full[h], R_DOWN)
                dve.tensor_tensor(half(x1, h), R[h][:, 0:HALF], half(res, h), ALU.add).then_inc(rows_out[h], 1)
                dve.wait_ge(rows_out[h], R_DOWN)
                stats(LNX1, h, half(x1, h))
                if h == 0:
                    take_epsilon(LNX1)
            mean_and_rstd(LNX1)
            apply(LNX1, [half(x1, 0), half(x1, 1)], x1)
            turned_lo_parts(T_X1)
            for h in range(2):
                dve.wait_ge(neigh_hi[h], 1)
                dve.tensor_tensor(nT_lo[:, 2 * h:2 * h + 2, :], two(U[h]), nT_hi[:, 2 * h:2 * h + 2, :].bitcast(F32),
                                  ALU.subtract).then_inc(neigh_out[h], 1)
            split_lo("neigh")
            split_lo("gin0")
            for h in range(2):
                dve.wait_ge(rows_full[h], R_L1)
                stats(LNH, h, R[h][:, 0:HALF])
                if h == 0:
                    take_epsilon(LNH)
            mean_and_variance(LNH)
            dve.wait_ge(res_ready, 2)
            for h in range(2):
                dve.scalar_tensor_tensor(half(xn, h), R[h][:, 0:HALF], mv[:, LNH, 0:1], row("gamma", h),
                                         ALU.subtract, ALU.mult).then_inc(rows_out[h], 1)
            dve.wait_ge(rstd_ready, LNH + 1)
            for h in range(2):
                dve.wait_ge(rows_out[h], R_L1)
                mark(dve.scalar_tensor_tensor(half(xn, h), half(xn, h), rstd[:, LNH:LNH + 1], half(res, h),
                                              ALU.mult, ALU.add))
            for h in range(2):
                dve.wait_ge(dve_step, done[0] - 1)
                stats(LNX2, h, half(xn, h))
            take_epsilon(LNX2)
            mean_and_rstd(LNX2)
            apply(LNX2, [half(xn, 0), half(xn, 1)], xn)
            for i in range(GIN):
                turned_lo_parts(T_GIN + i)
                for name in [["gin1", "gin2"], ["gin3"], ["gin4"], ["gcn"], []][i]:
                    split_lo(name)
            for h in range(2):
                dve.wait_ge(rows_full[h], R_GIN + GIN - 1)
                dve.tensor_tensor_reduce(half(h_sb, h), R[h][:, 0:HALF], zeros[:, :], 1.0, 0.0,
                                         ALU.add, ALU.max, half_max[:, h:h + 1]).then_inc(rows_out[h], 1)
                dve.wait_ge(rows_out[h], R_GIN + GIN - 1)
                if h == 1:
                    dve.scalar_tensor_tensor(lsm[:, 0:1], half_max[:, 0:1], half_max[:, 1:2], minus_one[:, :],
                                             ALU.max, ALU.mult).then_inc(max_ready, 1)
                mark(dve.scalar_tensor_tensor(half(xn, h), half(h_sb, h), 0.0, half(xn, h), ALU.max, ALU.add))
            dve.wait_ge(dve_step, done[0])
            for h in range(2):
                stats(LNX3, h, half(xn, h))
            take_epsilon(LNX3)
            mean_and_variance(LNX3)
            dve.wait_ge(lse_ready, 5)
            mark(dve.tensor_scalar(half(xn, 0), half(xn, 0), lsm[:, 3:4], None, ALU.add))
            mark(dve.tensor_tensor(mv[:, LNX3, 0:1], mv[:, LNX3, 0:1], lsm[:, 3:4], ALU.add))
            dve.wait_ge(dve_step, done[0])
            dve.wait_ge(rstd_ready, LNX3 + 1)
            apply(LNX3, [half(xn, 0), half(xn, 1)], xn, before_second=(shifted, 1))
            turned_lo_parts(T_X3)
            split_lo("dense")
            turned_lo_parts(T_AGG)
            dve.wait_ge(res_ready, 3)
            dve.wait_ge(rows_full[0], R_DENSE)
            link(dve.tensor_tensor(half(res, 0), U[0][:, 0:HALF], half(res, 0), ALU.add))
            stats(LNX4, 0, half(res, 0))
            dve.wait_ge(rows_full[1], R_DENSE)
            stats(LNX4, 1, U[1][:, 0:HALF])
            take_epsilon(LNX4)
            mean_and_rstd(LNX4)
            apply(LNX4, [half(res, 0), U[1][:, 0:HALF]], res)


def kernel(**inputs):
    import numpy as np
    import concourse.bacc as bacc
    from concourse.bass_utils import run_bass_kernel_spmd as run

    a = {k: np.asarray(v) for k, v in inputs.items()}
    w_in, w1, w2 = a["L0_gnn_w_in"], a["L0_gnn_w1"], a["L0_gnn_w2"]
    by_name = {"q": w_in[0:D].T, "k": w_in[D:2 * D].T, "v": w_in[2 * D:3 * D].T, "out": a["L0_gnn_w_out"].T,
               "self": a["L1_gnn_W_self"].T, "neigh": a["L1_gnn_W_neigh"].T, "gin0": a["L2_gnn_W1"],
               "gcn": a["L3_gnn_W_gcn"], "dense": a["L3_gnn_W_dense"]}
    for j in range(4):
        by_name[f"up{j}"] = w1[j * D:(j + 1) * D].T
        by_name[f"down{j}"] = w2.T[j * D:(j + 1) * D]
        by_name[f"gin{j + 1}"] = a["L2_gnn_Ws"][j]
    weights = np.stack([by_name[g].reshape(C, P, D).transpose(1, 0, 2) for g in GROUPS])
    b_in = a["L0_gnn_b_in"]
    columns = {"ln1_w": a["L0_gnn_ln1_w"], "ln1_b": a["L0_gnn_ln1_b"], "b_q": b_in[0:D], "b_k": b_in[D:2 * D],
               "b_up": a["L0_gnn_b1"]}
    cols = np.concatenate([columns[name].reshape(-1, P).T for name, _ in COLS], axis=1)
    all_rows = {"gamma": a["L1_gnn_gamma"], "beta": a["L1_gnn_beta"], "b_dense": a["L3_gnn_b_dense"]}
    rows = np.stack([all_rows[name] for name in ROWS])
    bias_rows = np.concatenate([b_in[2 * D:3 * D], a["L0_gnn_ln2_w"], a["L0_gnn_ln2_b"], a["L0_gnn_b_out"],
                                a["L0_gnn_b2"], a["L1_gnn_bias"], a["L2_gnn_b1"],
                                a["L2_gnn_bs"].reshape(-1), a["L3_gnn_b_gcn"],
                                a["L3_gnn_b_dense"]]).reshape(-1, D)
    edges = np.concatenate([a["src"].reshape(P, EC), a["dst"].reshape(P, EC)], axis=1)
    arrays = {"x": a["x"], "edges": edges, "cols": cols, "rows": rows, "bias_rows": bias_rows,
              "eps": a["L2_gnn_eps"], "weights": weights}
    arrays = {f"in_{k}": np.ascontiguousarray(v) for k, v in arrays.items()}

    nc = bacc.Bacc("TRN2", target_bir_lowering=False, num_devices=1)
    args = [nc.dram_tensor(k, v.shape, mybir.dt.from_np(v.dtype), kind="ExternalInput").ap()
            for k, v in arrays.items()]
    result = nc.dram_tensor("out_x", (P, D), F32, kind="ExternalOutput").ap()
    residual_gnn(nc, *args, result)
    got = run(nc, [arrays], core_ids=[0])
    return got.results[0]["out_x"]
```
